# Optimizing a Trainium2 kernel written in Bass

```python
import numpy as np
import jax
import jax.numpy as jnp

def _softmax(x, axis=-1):
    return jax.nn.softmax(x, axis=axis)

def _gelu(x):
    return jax.nn.gelu(x, approximate=True)

def _silu(x):
    return jax.nn.silu(x)

def _sigmoid(x):
    return jax.nn.sigmoid(x)

def _layernorm(x, axis=-1, eps=1e-05):
    m = jnp.mean(x, axis=axis, keepdims=True)
    v = jnp.var(x, axis=axis, keepdims=True)
    return (x - m) / jnp.sqrt(v + eps)

def _scatter_add(tgt, idx, src, axis=0):
    return tgt.at[idx].add(src)

def _segment_sum(src, seg, n):
    return jax.ops.segment_sum(src, seg, n)
kernel_name = 'mk_vit_tower_cls_d1_tok_img256_r4_778c12'

def setup_inputs(seed: int=0):
    np.random.seed(seed)
    _w = jnp.asarray

    def _rec_inputs():
        import jax
        import jax.numpy as jnp
        _rk = jax.random.key(seed)
        x = -0.000395706 + 0.999959 * jax.random.normal(jax.random.fold_in(_rk, 1), (32, 1, 224, 224), jnp.float32)
        cls_tok = 0.02 * jax.random.normal(jax.random.fold_in(_rk, 5), (1, 1, 64), jnp.float32)
        return (x, cls_tok)
    x, cls_tok = _rec_inputs()

    def _L0_tok_setup():
        import jax, jax.numpy as jnp
        import numpy as np
        IMAGE_SIZE = 224
        PATCH_SIZE = 7
        EMBED_DIM = 64
        NUM_PATCHES = (IMAGE_SIZE // PATCH_SIZE) ** 2
        PATCH_DIM = PATCH_SIZE ** 2
        key = jax.random.key(seed)
        kx, kw, kb, kp = jax.random.split(key, 4)
        x = jax.random.normal(kx, (64, 1, IMAGE_SIZE, IMAGE_SIZE), dtype=jnp.float32)
        bound = 1.0 / np.sqrt(PATCH_DIM)
        W = jax.random.uniform(kw, (EMBED_DIM, PATCH_DIM), minval=-bound, maxval=bound, dtype=jnp.float32)
        b = jax.random.uniform(kb, (EMBED_DIM,), minval=-bound, maxval=bound, dtype=jnp.float32)
        pos = jax.random.uniform(kp, (1, NUM_PATCHES, EMBED_DIM), dtype=jnp.float32)
        return {'x': x, 'W': W, 'b': b, 'pos': pos}
    _L0_tok_all = _L0_tok_setup()
    _L0_tok_in = {k: v for k, v in _L0_tok_all.items() if k in ('W', 'b', 'pos')}
    del _L0_tok_all

    def _L0_attn_setup():
        import jax, jax.numpy as jnp
        import numpy as np
        BSZ, L, D, S, K = (8, 1024, 64, 16, 4)
        key = jax.random.key(seed)
        ks = jax.random.split(key, 8)
        sc = 0.02
        return {'x': jax.random.normal(ks[0], (BSZ, L, D), jnp.float32), 'dt': jax.random.normal(ks[1], (D, S), jnp.float32) * 0.01, 'B_w': jax.random.normal(ks[2], (S, D), jnp.float32) * sc, 'C_w': jax.random.normal(ks[3], (D, S), jnp.float32) * sc, 'conv_w': jax.random.normal(ks[4], (D, 1, K), jnp.float32) * sc, 'conv_b': jnp.zeros((D,), jnp.float32), 'in_w': jax.random.normal(ks[5], (2 * D, D), jnp.float32) * sc, 'in_b': jnp.zeros((2 * D,), jnp.float32), 'out_w': jax.random.normal(ks[6], (D, D), jnp.float32) * sc, 'out_b': jnp.zeros((D,), jnp.float32), 'gamma': jnp.ones((D,), jnp.float32), 'beta': jnp.zeros((D,), jnp.float32)}
    _L0_attn_all = _L0_attn_setup()
    _L0_attn_in = {k: v for k, v in _L0_attn_all.items() if k in ('dt', 'B_w', 'C_w', 'conv_w', 'conv_b', 'in_w', 'in_b', 'out_w', 'out_b', 'gamma', 'beta')}
    del _L0_attn_all

    def _L0_ffn_setup():
        import jax, jax.numpy as jnp
        import numpy as np
        B, T, C = (64, 96, 64)
        NH, NKV = (4, 2)
        HD = C // NH
        NREP = NH // NKV
        NE, TOPK = (8, 2)
        HID = int(8 / 3 * C)
        EPS_RMS = 1e-06

        def _rope_tables(t_len):
            inv_freq = 1.0 / 10000.0 ** (np.arange(0, HD, 2, dtype=np.float32) / HD)
            t = np.arange(t_len, dtype=np.float32)
            freqs = np.outer(t, inv_freq)
            emb = np.concatenate([freqs, freqs], axis=-1)
            return (jnp.asarray(np.cos(emb)), jnp.asarray(np.sin(emb)))

        def _rotate_half(x):
            h = x.shape[-1] // 2
            return jnp.concatenate([-x[..., h:], x[..., :h]], axis=-1)

        def _rmsnorm(v, w):
            return v * jax.lax.rsqrt(jnp.mean(v * v, axis=-1, keepdims=True) + EPS_RMS) * w
        key = jax.random.key(seed)
        ks = jax.random.split(key, 10)
        s = lambda k, shape: jax.random.normal(k, shape, jnp.float32) * 0.02
        return {'x': jax.random.normal(ks[0], (B, T, C), jnp.float32), 'ln1_w': jnp.ones((C,), jnp.float32), 'ln2_w': jnp.ones((C,), jnp.float32), 'wq': s(ks[1], (NH * HD, C)), 'wk': s(ks[2], (NKV * HD, C)), 'wv': s(ks[3], (NKV * HD, C)), 'wo': s(ks[4], (C, C)), 'router_w': s(ks[5], (NE, C)), 'w1': s(ks[6], (NE, HID, C)), 'w2': s(ks[7], (NE, C, HID)), 'w3': s(ks[8], (NE, HID, C))}
    _L0_ffn_all = _L0_ffn_setup()
    _L0_ffn_in = {k: v for k, v in _L0_ffn_all.items() if k in ('ln1_w', 'ln2_w', 'wq', 'wk', 'wv', 'wo', 'router_w', 'w1', 'w2', 'w3')}
    del _L0_ffn_all
    return {'x': x, 'cls_tok': cls_tok, 'L0_tok_W': _L0_tok_in['W'], 'L0_tok_b': _L0_tok_in['b'], 'L0_tok_pos': _L0_tok_in['pos'], 'L0_attn_dt': _L0_attn_in['dt'], 'L0_attn_B_w': _L0_attn_in['B_w'], 'L0_attn_C_w': _L0_attn_in['C_w'], 'L0_attn_conv_w': _L0_attn_in['conv_w'], 'L0_attn_conv_b': _L0_attn_in['conv_b'], 'L0_attn_in_w': _L0_attn_in['in_w'], 'L0_attn_in_b': _L0_attn_in['in_b'], 'L0_attn_out_w': _L0_attn_in['out_w'], 'L0_attn_out_b': _L0_attn_in['out_b'], 'L0_attn_gamma': _L0_attn_in['gamma'], 'L0_attn_beta': _L0_attn_in['beta'], 'L0_ffn_ln1_w': _L0_ffn_in['ln1_w'], 'L0_ffn_ln2_w': _L0_ffn_in['ln2_w'], 'L0_ffn_wq': _L0_ffn_in['wq'], 'L0_ffn_wk': _L0_ffn_in['wk'], 'L0_ffn_wv': _L0_ffn_in['wv'], 'L0_ffn_wo': _L0_ffn_in['wo'], 'L0_ffn_router_w': _L0_ffn_in['router_w'], 'L0_ffn_w1': _L0_ffn_in['w1'], 'L0_ffn_w2': _L0_ffn_in['w2'], 'L0_ffn_w3': _L0_ffn_in['w3']}

def reference(x, cls_tok, L0_tok_W, L0_tok_b, L0_tok_pos, L0_attn_dt, L0_attn_B_w, L0_attn_C_w, L0_attn_conv_w, L0_attn_conv_b, L0_attn_in_w, L0_attn_in_b, L0_attn_out_w, L0_attn_out_b, L0_attn_gamma, L0_attn_beta, L0_ffn_ln1_w, L0_ffn_ln2_w, L0_ffn_wq, L0_ffn_wk, L0_ffn_wv, L0_ffn_wo, L0_ffn_router_w, L0_ffn_w1, L0_ffn_w2, L0_ffn_w3):
    import jax
    import jax.numpy as jnp

    def _L0_tok_ref(x, W, b, pos):
        import jax, jax.numpy as jnp
        import numpy as np
        IMAGE_SIZE = 224
        PATCH_SIZE = 7
        EMBED_DIM = 64
        NUM_PATCHES = (IMAGE_SIZE // PATCH_SIZE) ** 2
        PATCH_DIM = PATCH_SIZE ** 2
        B = x.shape[0]
        p = PATCH_SIZE
        n = IMAGE_SIZE // p
        patches = x.reshape(B, n, p, n, p).transpose(0, 1, 3, 2, 4).reshape(B, n * n, p * p)
        out = jnp.einsum('bnd,ed->bne', patches, W) + b + pos
        return out

    def _L0_attn_ref(x, dt, B_w, C_w, conv_w, conv_b, in_w, in_b, out_w, out_b, gamma, beta):
        import jax, jax.numpy as jnp
        import numpy as np
        BSZ, L, D, S, K = (8, 1024, 64, 16, 4)
        d_model = x.shape[-1]
        k = conv_w.shape[-1]
        xr = x @ in_w.T + in_b
        xp, res = jnp.split(xr, 2, axis=-1)
        xc = jnp.transpose(xp, (0, 2, 1))
        xc = jax.lax.conv_general_dilated(xc, conv_w, window_strides=(1,), padding=[(k - 1, 0)], feature_group_count=d_model, dimension_numbers=('NCH', 'OIH', 'NCH'))
        xc = xc + conv_b[None, :, None]
        xconv = jnp.transpose(xc, (0, 2, 1))
        dA = jnp.exp(jnp.einsum('bld,ds->bls', xconv, dt))
        dB = xconv @ B_w.T
        dA_cp = jnp.cumprod(dA, axis=1)
        yc = jnp.cumsum(dA_cp * dB, axis=1)
        y = jnp.concatenate([dB[:, :1], yc[:, 1:] - yc[:, :-1] * dA[:, 1:]], axis=1)
        y = y @ C_w.T
        out = y * jax.nn.silu(res) @ out_w.T + out_b
        out = out + xconv
        mean = out.mean(axis=(0, 1))
        var = jnp.mean((out - mean) ** 2, axis=(0, 1))
        out = (out - mean) * jax.lax.rsqrt(var + 1e-05) * gamma + beta
        return out

    def _L0_ffn_ref(x, ln1_w, ln2_w, wq, wk, wv, wo, router_w, w1, w2, w3):
        import jax, jax.numpy as jnp
        import numpy as np
        B, T, C = (64, 96, 64)
        NH, NKV = (4, 2)
        HD = C // NH
        NREP = NH // NKV
        NE, TOPK = (8, 2)
        HID = int(8 / 3 * C)
        EPS_RMS = 1e-06

        def _rope_tables(t_len):
            inv_freq = 1.0 / 10000.0 ** (np.arange(0, HD, 2, dtype=np.float32) / HD)
            t = np.arange(t_len, dtype=np.float32)
            freqs = np.outer(t, inv_freq)
            emb = np.concatenate([freqs, freqs], axis=-1)
            return (jnp.asarray(np.cos(emb)), jnp.asarray(np.sin(emb)))

        def _rotate_half(x):
            h = x.shape[-1] // 2
            return jnp.concatenate([-x[..., h:], x[..., :h]], axis=-1)

        def _rmsnorm(v, w):
            return v * jax.lax.rsqrt(jnp.mean(v * v, axis=-1, keepdims=True) + EPS_RMS) * w
        Bx, Tx, Cx = x.shape
        h = _rmsnorm(x, ln1_w)
        q = (h @ wq.T).reshape(Bx, Tx, NH, HD).transpose(0, 2, 1, 3)
        k = (h @ wk.T).reshape(Bx, Tx, NKV, HD).transpose(0, 2, 1, 3)
        v = (h @ wv.T).reshape(Bx, Tx, NKV, HD).transpose(0, 2, 1, 3)
        cos, sin = _rope_tables(Tx)
        cos, sin = (cos[None, None], sin[None, None])
        q = q * cos + _rotate_half(q) * sin
        k = k * cos + _rotate_half(k) * sin
        k = jnp.repeat(k, NREP, axis=1)
        v = jnp.repeat(v, NREP, axis=1)
        scores = jnp.einsum('bhtd,bhsd->bhts', q, k) / jnp.sqrt(jnp.float32(HD))
        causal = jnp.tril(jnp.ones((Tx, Tx), dtype=bool))
        scores = jnp.where(causal[None, None], scores, jnp.float32(-1e+30))
        att = jax.nn.softmax(scores, axis=-1)
        y = jnp.einsum('bhts,bhsd->bhtd', att, v).transpose(0, 2, 1, 3).reshape(Bx, Tx, Cx)
        x = x + y @ wo.T
        flat = _rmsnorm(x, ln2_w).reshape(-1, Cx)
        probs = jax.nn.softmax(flat @ router_w.T, axis=-1)
        tp, ti = jax.lax.top_k(probs, TOPK)
        tp = tp / (jnp.sum(tp, axis=-1, keepdims=True) + 1e-09)
        weights = jnp.sum(tp[..., None] * jax.nn.one_hot(ti, NE, dtype=flat.dtype), axis=1)
        out = jnp.zeros_like(flat)
        for e in range(NE):
            hh = jax.nn.silu(flat @ w1[e].T) * (flat @ w3[e].T)
            out = out + weights[:, e:e + 1] * (hh @ w2[e].T)
        return x + out.reshape(Bx, Tx, Cx)
    h = _L0_tok_ref(x, L0_tok_W, L0_tok_b, L0_tok_pos)
    h = jnp.concatenate([jnp.broadcast_to(cls_tok, (h.shape[0], 1, h.shape[2])), h], axis=1)
    h = h + _L0_attn_ref(_layernorm(h, axis=-1), L0_attn_dt, L0_attn_B_w, L0_attn_C_w, L0_attn_conv_w, L0_attn_conv_b, L0_attn_in_w, L0_attn_in_b, L0_attn_out_w, L0_attn_out_b, L0_attn_gamma, L0_attn_beta)
    h = h + _L0_ffn_ref(_layernorm(h, axis=-1), L0_ffn_ln1_w, L0_ffn_ln2_w, L0_ffn_wq, L0_ffn_wk, L0_ffn_wv, L0_ffn_wo, L0_ffn_router_w, L0_ffn_w1, L0_ffn_w2, L0_ffn_w3)
    return h

_drawn_inputs = setup_inputs


def setup_inputs(seed=0):
    import zlib

    import numpy as np

    out = dict(_drawn_inputs(seed))
    spreads = {'L0_attn_conv_b': (0.0, 0.1),
     'L0_attn_in_b': (0.0, 0.1),
     'L0_attn_out_b': (0.0, 0.8),
     'L0_attn_gamma': (1.0, 0.2),
     'L0_attn_beta': (0.0, 0.1),
     'L0_ffn_ln1_w': (1.0, 0.6),
     'L0_ffn_ln2_w': (1.0, 0.6)}
    factors = {'L0_ffn_wq': 8.0,
     'L0_ffn_wk': 8.0,
     'L0_ffn_wv': 8.0,
     'L0_ffn_wo': 8.0,
     'L0_ffn_router_w': 8.0,
     'L0_ffn_w1': 8.0,
     'L0_ffn_w2': 8.0,
     'L0_ffn_w3': 8.0}
    for name, (base, spread) in spreads.items():
        noise = np.random.default_rng([zlib.crc32(name.encode()), seed]).standard_normal(out[name].shape)
        drawn = base * np.exp(spread * noise) if base else spread * noise
        out[name] = jnp.asarray(drawn.astype(out[name].dtype))
    for name, factor in factors.items():
        out[name] = (out[name] * factor).astype(out[name].dtype)
    return out
```

```python
from contextlib import ExitStack

import concourse.bass as bass
from concourse import mybir

F32 = mybir.dt.float32
BF16 = mybir.dt.bfloat16
F16 = mybir.dt.float16
ALU = mybir.AluOpType
ACT = mybir.ActivationFunctionType
AX_X = mybir.AxisListType.X

P = 128
D = 64
IMG, PATCH = 224, 7
GRID = IMG // PATCH
PIX = PATCH * PATCH
L = GRID * GRID
T = L + 1
TP = T + 1
THIRD = TP // 3
STATE = 16
TAPS = 4
NH, NKV, HD = 4, 2, 16
QK = (NH + NKV) * HD
TILES = 8
NE, HID = 8, 170
PAIRS = NE // 2
CHUNKS = ((0, 114), (228, 112), (114, 114))
X_SCALE, W_TOP = 2.0 ** 12, 2.0 ** 14
LN_EPS, RMS_EPS, BN_EPS = 1e-5, 1e-6, 1e-5
MASKED = -1e30
XCOLS = IMG - PATCH + 1

C_IDENT = 0
C_MEAN = C_IDENT + P
C_HALF = C_MEAN + P
C_FOLD = C_HALF + P
C_DEN = C_FOLD + P
C_MASK_Q = C_DEN + P
C_MASK_K = C_MASK_Q + P
C_SPREAD = C_MASK_K + P
C_FIRST = C_SPREAD + 2 * PAIRS * P
C_COS = C_FIRST + 9 * 2 * NE
C_SIN = C_COS + TP
C_END = C_SIN + TP

AHEAD = 3


def thirds(ap):
    return ap.rearrange("p (c n) -> p c n", c=3)


def shape_constants():
    import numpy as np

    c = np.zeros((P, C_END), np.float32)
    eye = np.eye(P, dtype=np.float32)
    half = np.arange(P) // D
    c[:, C_IDENT:C_IDENT + P] = eye
    c[:, C_MEAN:C_MEAN + P] = (half[:, None] == half[None, :]) / D
    c[:, C_HALF:C_HALF + P] = 0.5 * (np.arange(P)[:, None] % D == np.arange(P)[None, :] % D)
    same = (np.arange(P)[:, None] % D == np.arange(D)[None, :]).astype(np.float32)
    c[:, C_FOLD:C_FOLD + D] = same
    c[:, C_DEN:C_DEN + P] = np.arange(P)[:, None] == 32 * (np.arange(P)[None, :] // 32) + HD
    later = np.arange(P)[None, :] > np.arange(P)[:, None]
    c[:, C_MASK_Q:C_MASK_Q + P] = np.where(later, MASKED, 0)
    c[:, C_MASK_K:C_MASK_K + P] = np.where(later.T, MASKED, 0)
    for b in range(2):
        for p in range(PAIRS):
            for part in range(3):
                for m in range(P):
                    c[part * 32 + b * NE + 2 * p + m // D, C_SPREAD + (b * PAIRS + p) * P + m] = 1
    c[:, C_FIRST:C_COS] = np.tile(NE - np.arange(NE), 9 * 2)
    inv_freq = 1.0 / 10000.0 ** (np.arange(0, HD, 2, dtype=np.float32) / HD)
    freqs = np.outer(np.arange(TP, dtype=np.float32), inv_freq.astype(np.float32))
    cos, sin = np.cos(freqs).T, np.sin(freqs).T
    c[0:QK, C_COS:C_COS + TP] = np.tile(cos, (2 * (NH + NKV), 1))
    c[0:QK, C_SIN:C_SIN + TP] = np.tile(np.concatenate([-sin, sin]), (NH + NKV, 1))
    return c


class Chip:

    def __init__(self, nc, ctx, images):
        def sb(name, cols, dt=F32):
            return ctx.enter_context(nc.sbuf_tensor(name, [P, cols], dt))

        self.consts = sb("consts", C_END)
        self.vec = sb("vec", 32)
        self.pos = sb("pos", TP)
        self.tok_w = sb("tok_w", P)
        self.in_p = sb("in_p", P)
        self.in_r = sb("in_r", P)
        self.out_w = sb("out_w", P)
        self.taps = sb("taps", TAPS * P)
        self.dt_w = sb("dt_w", 2 * STATE)
        self.b_w = sb("b_w", 2 * STATE)
        self.c_w = sb("c_w", P)
        self.qk_w = sb("qk_w", QK)
        self.qk_swapped = sb("qk_swapped", QK)
        self.v_w = sb("v_w", NKV * HD)
        self.o_w = sb("o_w", D)
        self.router = sb("router", 2 * NE)
        self.w1 = sb("w1", 2 * PAIRS * 3 * P, F16)
        self.w3 = sb("w3", 2 * PAIRS * 3 * P, F16)
        self.unscale = sb("unscale", 2)
        self.w2 = sb("w2", PAIRS * 3 * P)
        self.ident16 = sb("ident16", P, BF16)
        self.mask_q16 = sb("mask_q16", P, BF16)
        self.mask_k16 = sb("mask_k16", P, BF16)
        self.spread16 = sb("spread16", 2 * PAIRS * P, BF16)
        self.stats = sb("stats", (images // 2) * 3 * 6)
        self.psum = ctx.enter_context(nc.psum_tensor("psum", [P, 8, 512], F32))
        self.bank = [self.psum[:, i, :] for i in range(8)]

    def thirds(self, first):
        return self.psum[:, first:first + 3, 0:THIRD]

    def const(self, at, n=P):
        return self.consts[:, at:at + n]

    def v(self, name):
        i = VEC.index(name)
        return self.vec[:, i:i + 1]


VEC = ["tok_b", "in_b_p", "in_b_r", "conv_b", "out_b", "gamma", "beta", "ln1", "ln2",
       "tap0", "tap1", "tap2", "tap3", "ln_eps", "rms_eps", "bn_a", "bn_b", "cls"]


def load_weights(nc, chip, dram):
    consts, vec = chip.consts, chip.vec
    with ExitStack() as ctx:
        def sem(name):
            return ctx.enter_context(nc.semaphore(name))

        def natural(name, cols):
            return ctx.enter_context(nc.sbuf_tensor("nat_" + name, [P, cols], F32))

        n_small = natural("small", 9 * P)
        tok, in_p, in_r, out_w, qk, qk_s, v_o, router, b_w = (
            n_small[:, i * P:(i + 1) * P] for i in range(9))
        n_o = natural("o", P)
        n_c = natural("c", 2 * STATE)
        n_pos = natural("pos", TILES * P)
        n_w1 = natural("w1", PAIRS * 3 * P)
        n_w3 = natural("w3", PAIRS * 3 * P)
        n_w2 = natural("w2", PAIRS * 2 * HID)
        w1, w3 = natural("w1_turned", PAIRS * 3 * P), natural("w3_turned", PAIRS * 3 * P)
        ones, largest, smallest, scale, peak, diag = (natural(x, n) for x, n in (
            ("ones", P), ("largest", 2), ("smallest", 2), ("scale", 2), ("peak", 1), ("diag", 2)))

        cleared = [n_small[:, :], n_o[:, :], n_c[:, :], n_w2[:, :], chip.dt_w[:, :], w1[:, :], w3[:, :],
                   chip.w2[:, :], chip.pos[:, :], chip.v("ln_eps"), chip.v("rms_eps"), ones[:, :]]
        values = {9: LN_EPS, 10: RMS_EPS, 11: 1.0}

        turns = [
            (tok, chip.tok_w[:, :], None),
            (in_p, chip.in_p[:, :], None),
            (in_r, chip.in_r[:, :], None),
            (out_w, chip.out_w[:, :], None),
            (qk[0:QK, :], chip.qk_w[:, :], "ln1"),
            (qk_s[0:QK, :], chip.qk_swapped[:, :], "ln1"),
            (v_o[0:NKV * HD, :], chip.v_w[:, :], "ln1"),
            (n_o[0:D, :], chip.o_w[:, :], None),
            (router[0:2 * NE, :], chip.router[:, :], "ln2"),
            (b_w[0:2 * STATE, :], chip.b_w[:, :], None),
            (n_c[:, :], chip.c_w[0:2 * STATE, :], None),
        ]
        turns += [(n_pos[:, j * P:(j + 1) * P], chip.pos[:, 1 + j * P:1 + (j + 1) * P], "tok_b")
                  for j in range(TILES)]
        for i in range(PAIRS * 3):
            first, rows = CHUNKS[i % 3]
            for n, w in ((n_w1, w1), (n_w3, w3)):
                turns.append((n[0:rows, i * P:(i + 1) * P], w[:, i * P:i * P + rows], "ln2"))
            at = i // 3 * 2 * HID + first
            turns.append((n_w2[:, at:at + rows], chip.w2[0:rows, i * P:(i + 1) * P], None))

        cleared_all = sem("cleared_all")
        loaded = sem("loaded")
        turned = sem("turned")
        copied = sem("copied")
        scaled = sem("scaled")
        peaks = sem("peaks")
        bank = chip.bank

        def w_dram(name, m):
            w = dram[name]
            return bass.AP(w.tensor, CHUNKS[m][0] * D, [[D, CHUNKS[m][1]], [2 * HID * D, PAIRS], [1, D]])

        def column(name, n=D, step=1, offset=0):
            return bass.AP(dram[name].tensor, offset, [[step, n], [1, 1]])

        loads = [(consts[:, :], dram["shape_consts"])]
        for b in range(2):
            r = slice(D * b, D * (b + 1))
            e = slice(NE * b, NE * (b + 1))
            s = slice(STATE * b, STATE * (b + 1))
            loads += [
                (tok[r, D * b:D * b + PIX], dram["L0_tok_W"]),
                (in_p[r, r], dram["L0_attn_in_w"][0:D, :]),
                (in_r[r, r], dram["L0_attn_in_w"][D:2 * D, :]),
                (out_w[r, r], dram["L0_attn_out_w"]),
                (router[e, r], dram["L0_ffn_router_w"]),
                (b_w[s, r], dram["L0_attn_B_w"]),
                (n_c[r, s], dram["L0_attn_C_w"]),
                (chip.dt_w[r, s], dram["L0_attn_dt"]),
                (n_pos[:, :].rearrange("p (j u d) -> p j u d", j=TILES, u=2)[:, :, b, :],
                 dram["L0_tok_pos"][0].rearrange("(j p) d -> p j d", p=P)),
                (vec[r, 9:13], dram["L0_attn_conv_w"].rearrange("d a k -> d (a k)")),
            ]
            loads += [(vec[r, VEC.index(v):VEC.index(v) + 1], column(*src)) for v, src in {
                "tok_b": ("L0_tok_b",), "in_b_p": ("L0_attn_in_b",), "in_b_r": ("L0_attn_in_b", D, 1, D),
                "conv_b": ("L0_attn_conv_b",), "out_b": ("L0_attn_out_b",), "gamma": ("L0_attn_gamma",),
                "beta": ("L0_attn_beta",), "ln1": ("L0_ffn_ln1_w",), "ln2": ("L0_ffn_ln2_w",),
                "cls": ("cls_tok",)}.items()]
            for n, name in ((n_w1, "L0_ffn_w1"), (n_w3, "L0_ffn_w3")):
                to = n[:, :].rearrange("p (q m u d) -> p q m u d", q=PAIRS, m=3, u=2)
                loads += [(to[0:CHUNKS[m][1], :, m, b, :], w_dram(name, m)) for m in range(3)]
            loads.append((n_w2[r, :].rearrange("c (q u h) -> c q u h", q=PAIRS, u=2)[:, :, b, :],
                          bass.AP(dram["L0_ffn_w2"].tensor, b * D * HID,
                                  [[HID, D], [2 * D * HID, PAIRS], [1, HID]])))
        loads += [(qk[0:NH * HD, 0:D], dram["L0_ffn_wq"]), (qk[NH * HD:QK, 0:D], dram["L0_ffn_wk"]),
                  (v_o[0:NKV * HD, 0:D], dram["L0_ffn_wv"])]
        for h in range(NH + NKV):
            w, g = (dram["L0_ffn_wq"], h) if h < NH else (dram["L0_ffn_wk"], h - NH)
            half = HD // 2
            loads += [(qk_s[HD * h:HD * h + half, 0:D], w[HD * g + half:HD * (g + 1), :]),
                      (qk_s[HD * h + half:HD * (h + 1), 0:D], w[HD * g:HD * g + half, :])]
        loads.append((n_o[0:D, :].rearrange("o (h r) -> o h r", h=NH)[:, :, 0:HD],
                      dram["L0_ffn_wo"].rearrange("o (h r) -> o h r", h=NH)))

        block = ctx.enter_context(nc.Block())

        @block.gpsimd
        def _(pool):
            for i, ap in enumerate(cleared):
                pool.memset(ap, values.get(i, 0.0)).then_inc(cleared_all, 1)

        @block.sync
        def _(sp):
            sp.wait_ge(cleared_all, len(cleared))
            for to, src in loads[0::2]:
                sp.dma_start(to, src).then_inc(loaded, 16)

        @block.scalar
        def _(act):
            act.wait_ge(cleared_all, len(cleared))
            for to, src in loads[1::2]:
                act.dma_start(to, src).then_inc(loaded, 16)

        @block.tensor
        def _(pe):
            pe.wait_ge(cleared_all, len(cleared))
            pe.wait_ge(loaded, 16 * len(loads))
            for i, (src, _, _) in enumerate(turns):
                rows, cols = src.shape
                if i >= 8:
                    pe.wait_ge(copied, i - 7)
                pe.transpose(bank[i % 8][0:cols, 0:rows], src, chip.const(C_IDENT)[0:rows, 0:rows])\
                    .then_inc(turned, 1)
            pe.wait_ge(scaled, 5)
            pe.wait_ge(copied, len(turns))
            pe.transpose(bank[0][0:2, 0:P], largest[:, :], chip.const(C_IDENT)).then_inc(peaks, 1)
            pe.wait_ge(scaled, 7)
            pe.matmul(bank[1][:, 0:2], ones[0:2, :], diag[0:2, :], start=True, stop=True).then_inc(peaks, 1)

        @block.vector
        def _(dve):
            dve.wait_ge(cleared_all, len(cleared))
            dve.wait_ge(loaded, 16 * len(loads))
            for i, (src, to, by) in enumerate(turns):
                rows, cols = src.shape
                got = bank[i % 8][0:cols, 0:rows]
                dve.wait_ge(turned, i + 1)
                if by is None:
                    ins = dve.tensor_copy(to, got)
                else:
                    ins = dve.tensor_scalar(to, got, chip.v(by), None, ALU.add if by == "tok_b" else ALU.mult)
                ins.then_inc(copied, 1)
            n = len(turns)
            dve.tensor_copy(chip.pos[:, 0:1], chip.v("cls")).then_inc(copied, 1)
            for to, at in ((chip.ident16, C_IDENT), (chip.mask_q16, C_MASK_Q), (chip.mask_k16, C_MASK_K)):
                dve.tensor_copy(to[:, :], chip.const(at)).then_inc(copied, 1)
            dve.tensor_copy(chip.spread16[:, :], chip.const(C_SPREAD, 2 * PAIRS * P)).then_inc(copied, 1)
            for k in range(TAPS):
                dve.tensor_scalar(chip.taps[:, k * P:(k + 1) * P], chip.const(C_IDENT), chip.v(f"tap{k}"), None,
                                  ALU.mult).then_inc(copied, 1)
            dve.wait_ge(copied, n + 5 + TAPS)

            for k, w in enumerate((w1, w3)):
                dve.tensor_reduce(largest[:, k:k + 1], w[:, :], AX_X, ALU.max).then_inc(scaled, 1)
                dve.tensor_reduce(smallest[:, k:k + 1], w[:, :], AX_X, ALU.min).then_inc(scaled, 1)
            dve.wait_ge(scaled, 4)
            dve.scalar_tensor_tensor(largest[:, :], smallest[:, :], -1.0, largest[:, :], ALU.mult, ALU.max)\
               .then_inc(scaled, 1)
            dve.wait_ge(peaks, 1)
            dve.tensor_reduce(peak[0:2, :], bank[0][0:2, 0:P], AX_X, ALU.max).then_inc(scaled, 1)
            dve.wait_ge(scaled, 6)
            dve.tensor_scalar(diag[0:2, :], chip.const(C_IDENT)[0:2, 0:2], peak[0:2, :], None, ALU.mult)\
               .then_inc(scaled, 1)
            dve.wait_ge(peaks, 2)
            dve.tensor_scalar(largest[:, :], bank[1][:, 0:2], 1e-30, None, ALU.max).then_inc(scaled, 1)
            dve.wait_ge(scaled, 8)
            dve.reciprocal(scale[:, :], largest[:, :]).then_inc(scaled, 1)
            dve.tensor_scalar(chip.unscale[:, :], largest[:, :], 1.0 / (W_TOP * X_SCALE), None, ALU.mult)\
               .then_inc(scaled, 1)
            dve.wait_ge(scaled, 9)
            dve.tensor_scalar(scale[:, :], scale[:, :], W_TOP, None, ALU.mult).then_inc(scaled, 1)
            dve.wait_ge(scaled, 11)
            for k, (w, to) in enumerate(((w1, chip.w1), (w3, chip.w3))):
                half = PAIRS * 3 * P
                by = scale[:, k:k + 1]
                dve.tensor_scalar(to[:, 0:half], w[:, :], by, None, ALU.mult).then_inc(scaled, 1)
                dve.wait_ge(scaled, 12 + 2 * k)
                dve.scalar_tensor_tensor(to[:, half:], w[:, :], by, to[:, 0:half], ALU.mult, ALU.subtract)\
                   .then_inc(scaled, 1)
            dve.wait_ge(scaled, 15)


def mix(nc, chip, dram, images):
    turns = images // 4
    h_dram, o_dram = dram["h"], dram["mixed"]
    bank = chip.bank
    with ExitStack() as ctx:
        def sem(name):
            return ctx.enter_context(nc.semaphore(name))

        def two(name, cols):
            return [ctx.enter_context(nc.sbuf_tensor(f"{name}{k}", [P, cols], F32)) for k in range(2)]

        pixels, h, xc, sq, rstd, u = two("pixels", GRID * XCOLS), two("h", TP), two("xc", TP), two("sq", TP), \
            two("rstd", TP), two("u", TP)
        gate, xp, xconv, o = two("gate", TP), two("xp", TP + TAPS - 1), two("xconv", TP), two("o", TP)
        decay, scan = two("decay", TP), two("scan", TP)
        g, states, y = sq, rstd, xc
        ones = ctx.enter_context(nc.sbuf_tensor("ones", [P, TP], F32))
        S = 2 * STATE

        pixels_cleared = sem("pixels_cleared")
        preset = sem("preset")
        pixels_loaded = [sem("pixels_loaded0"), sem("pixels_loaded1")]
        h_stored = [sem("h_stored0"), sem("h_stored1")]
        o_stored = [sem("o_stored0"), sem("o_stored1")]
        names = """embedded h_ready mean_ready xc_ready sq_ready var_ready log_ready rstd_ready u_ready
            res_ready gate_ready xp_summed xp_ready conv_summed xconv_ready dt_ready decay_ready b_ready
            scan_ready bx_ready first_ready states_ready carried_ready y_ready c_ready g_ready out_ready
            o_ready stats_ready""".split()
        s = {name: sem(name) for name in names}

        def load(sp, i, k):
            for b in range(2):
                for p in range(PATCH):
                    first = (4 * i + 2 * k + b) * (IMG * IMG) + p * IMG
                    src = bass.AP(dram["x"].tensor, first, [[1, PATCH], [PATCH * IMG, GRID], [1, XCOLS]])
                    to = pixels[k][D * b + PATCH * p:D * b + PATCH * (p + 1), :]
                    sp.dma_start(to.rearrange("r (n c) -> r n c", n=GRID), src).then_inc(pixels_loaded[k], 16)

        block = ctx.enter_context(nc.Block())

        @block.sync
        def _(sp):
            def store(i):
                for ready, stored, tile, to in (("h_ready", h_stored, h, h_dram), ("o_ready", o_stored, o, o_dram)):
                    for k in range(2):
                        sp.wait_ge(s[ready], 2 * i + k + 1)
                        sp.dma_start(bass.AP(to.tensor, (4 * i + 2 * k) * (D * TP), [[TP, P], [1, TP]]),
                                     tile[k][:, :]).then_inc(stored[k], 16)

            for k in range(2):
                sp.wait_ge(pixels_cleared, 2)
                load(sp, 0, k)
            if turns > 1:
                with sp.Fori(0, turns - 1) as i:
                    for k in range(2):
                        sp.wait_ge(s["embedded"], 2 * i + k + 1)
                        load(sp, i + 1, k)
                    store(i)
            store(turns - 1)
            for k in range(2):
                sp.wait_ge(h_stored[k], 16 * turns)
                sp.wait_ge(o_stored[k], 16 * turns)

        @block.gpsimd
        def _(pool):
            pool.memset(pixels[0][:, :], 0.0).then_inc(pixels_cleared, 1)
            pool.memset(ones[:, :], 1.0).then_inc(preset, 1)
            for k in range(2):
                pool.memset(xp[k][:, 0:TAPS - 1], 0.0).then_inc(preset, 1)

        @block.scalar
        def _(act):
            act.wait_ge(preset, 3)
            with act.Fori(0, turns) as i:
                n = [act.snap(2 * i + k + 1) for k in range(2)]
                for k in range(2):
                    act.wait_ge(s["xc_ready"], n[k])
                    act.activation(sq[k][:, :], xc[k][:, :], ACT.Square).then_inc(s["sq_ready"], 1)
                for k in range(2):
                    act.wait_ge(s["var_ready"], n[k])
                    act.activation(thirds(rstd[k][:, :]), chip.thirds(3 * k), ACT.Ln,
                                   bias=chip.v("ln_eps")).then_inc(s["log_ready"], 1)
                for k in range(2):
                    act.wait_ge(s["log_ready"], n[k])
                    act.activation(rstd[k][:, :], rstd[k][:, :], ACT.Exp, scale=-0.5).then_inc(s["rstd_ready"], 1)
                for k in range(2):
                    act.wait_ge(s["res_ready"], n[k])
                    act.activation(thirds(gate[k][:, :]), chip.thirds(3 * k), ACT.Silu,
                                   bias=chip.v("in_b_r")).then_inc(s["gate_ready"], 1)
                for k in range(2):
                    act.wait_ge(s["xp_summed"], n[k])
                    act.activation(thirds(xp[k][:, TAPS - 1:]), chip.thirds(3 * k), ACT.Identity,
                                   bias=chip.v("in_b_p")).then_inc(s["xp_ready"], 1)
                for k in range(2):
                    act.wait_ge(s["conv_summed"], n[k])
                    act.activation(thirds(xconv[k][:, :]), chip.thirds(3 * k), ACT.Identity,
                                   bias=chip.v("conv_b")).then_inc(s["xconv_ready"], 1)
                for k in range(2):
                    act.wait_ge(s["dt_ready"], n[k])
                    act.activation(thirds(decay[k][0:S, :]), chip.thirds(3 * k)[0:S], ACT.Exp)\
                       .then_inc(s["decay_ready"], 1)

        @block.vector
        def _(dve):
            dve.memset(pixels[1][:, :], 0.0).then_inc(pixels_cleared, 1)
            dve.wait_ge(preset, 3)
            for k in range(2):
                dve.tensor_copy(h[k][:, 0:1], chip.pos[:, 0:1]).then_inc(preset, 1)
                dve.tensor_copy(h[k][:, T:TP], chip.pos[:, T:TP]).then_inc(preset, 1)
            dve.wait_ge(preset, 7)
            with dve.Fori(0, turns) as i:
                n = [dve.snap(2 * i + k + 1) for k in range(2)]
                for k in range(2):
                    dve.wait_ge(s["embedded"], n[k])
                    dve.wait_ge(h_stored[k], 16 * i)
                    dve.tensor_tensor(h[k][:, 1:T].rearrange("p (c n) -> p c n", c=2),
                                      chip.psum[:, 3 * k:3 * k + 2, :],
                                      chip.pos[:, 1:T].rearrange("p (c n) -> p c n", c=2), ALU.add)\
                       .then_inc(s["h_ready"], 1)
                for k in range(2):
                    dve.wait_ge(s["mean_ready"], n[k])
                    dve.tensor_tensor(thirds(xc[k][:, :]), thirds(h[k][:, :]), chip.thirds(3 * k), ALU.subtract)\
                       .then_inc(s["xc_ready"], 1)
                for k in range(2):
                    dve.wait_ge(s["rstd_ready"], n[k])
                    dve.tensor_tensor(u[k][:, :], xc[k][:, :], rstd[k][:, :], ALU.mult).then_inc(s["u_ready"], 1)
                for k in range(2):
                    dve.wait_ge(s["decay_ready"], n[k])
                    dve.tensor_tensor_scan(scan[k][0:S, :], decay[k][0:S, :], ones[0:S, :], 1.0, ALU.mult, ALU.mult)\
                       .then_inc(s["scan_ready"], 1)
                for k in range(2):
                    dve.wait_ge(s["b_ready"], n[k])
                    dve.wait_ge(s["scan_ready"], n[k])
                    dve.tensor_tensor(thirds(scan[k][0:S, :]), thirds(scan[k][0:S, :]),
                                      chip.thirds(3 * k)[0:S], ALU.mult).then_inc(s["bx_ready"], 1)
                    dve.tensor_copy(y[k][0:S, 0:1], chip.bank[3 * k][0:S, 0:1]).then_inc(s["first_ready"], 1)
                for k in range(2):
                    dve.wait_ge(s["bx_ready"], n[k])
                    dve.tensor_tensor_scan(states[k][0:S, :], ones[0:S, :], scan[k][0:S, :], 0.0, ALU.mult, ALU.add)\
                       .then_inc(s["states_ready"], 1)
                for k in range(2):
                    dve.wait_ge(s["states_ready"], n[k])
                    dve.tensor_tensor(scan[k][0:S, 1:TP], states[k][0:S, 0:TP - 1], decay[k][0:S, 1:TP], ALU.mult)\
                       .then_inc(s["carried_ready"], 1)
                for k in range(2):
                    dve.wait_ge(s["carried_ready"], n[k])
                    dve.wait_ge(s["first_ready"], n[k])
                    dve.tensor_tensor(y[k][0:S, 1:TP], states[k][0:S, 1:TP], scan[k][0:S, 1:TP], ALU.subtract)\
                       .then_inc(s["y_ready"], 1)
                for k in range(2):
                    dve.wait_ge(s["c_ready"], n[k])
                    dve.wait_ge(s["gate_ready"], n[k])
                    dve.tensor_tensor(thirds(g[k][:, :]), chip.thirds(3 * k), thirds(gate[k][:, :]), ALU.mult)\
                       .then_inc(s["g_ready"], 1)
                for k in range(2):
                    dve.wait_ge(s["out_ready"], n[k])
                    dve.wait_ge(s["xconv_ready"], n[k])
                    dve.wait_ge(o_stored[k], 16 * i)
                    dve.scalar_tensor_tensor(thirds(o[k][:, :]), chip.thirds(3 * k), chip.v("out_b"),
                                             thirds(xconv[k][:, :]), ALU.add, ALU.add).then_inc(s["o_ready"], 1)
                for k in range(2):
                    dve.wait_ge(s["o_ready"], n[k])
                    for c in range(3):
                        part = o[k][:, c * THIRD:min((c + 1) * THIRD, T)]
                        at = (2 * i + k) * 18 + 6 * c
                        ins = dve.bn_stats(chip.stats[:, bass.ds(at, 6)], part)
                    ins.then_inc(s["stats_ready"], 1)

        @block.tensor
        def _(pe):
            pe.wait_ge(preset, 3)

            def product(k, w, x, rows=P, contracted=P, shift=0, start=True, stop=True):
                for c in range(3):
                    ins = pe.matmul(chip.bank[3 * k + c][0:rows, 0:THIRD], w[0:contracted],
                                    x[0:contracted, c * THIRD + shift:(c + 1) * THIRD + shift],
                                    start=start, stop=stop)
                return ins

            with pe.Fori(0, turns) as i:
                n = [pe.snap(2 * i + k + 1) for k in range(2)]
                for k in range(2):
                    pe.wait_ge(pixels_loaded[k], (i + 1) * (2 * PATCH * 16))
                    pe.wait_ge(s["o_ready"], 2 * i)
                    for c in range(2):
                        view = pixels[k][:, :].rearrange("r (n c) -> r n c", n=GRID)
                        ins = pe.matmul(chip.bank[3 * k + c], chip.tok_w[:, :],
                                        view[:, c * GRID // 2:(c + 1) * GRID // 2, 0:XCOLS:PATCH],
                                        start=True, stop=True)
                    ins.then_inc(s["embedded"], 1)
                for k in range(2):
                    pe.wait_ge(s["h_ready"], n[k])
                    product(k, chip.const(C_MEAN), h[k]).then_inc(s["mean_ready"], 1)
                for k in range(2):
                    pe.wait_ge(s["sq_ready"], n[k])
                    product(k, chip.const(C_MEAN), sq[k]).then_inc(s["var_ready"], 1)
                for k in range(2):
                    pe.wait_ge(s["u_ready"], n[k])
                    product(k, chip.in_r[:, :], u[k]).then_inc(s["res_ready"], 1)
                for k in range(2):
                    pe.wait_ge(s["gate_ready"], n[k])
                    product(k, chip.in_p[:, :], u[k]).then_inc(s["xp_summed"], 1)
                for k in range(2):
                    pe.wait_ge(s["xp_ready"], n[k])
                    for c in range(3):
                        for t in range(TAPS):
                            ins = pe.matmul(chip.bank[3 * k + c][:, 0:THIRD], chip.taps[:, t * P:(t + 1) * P],
                                            xp[k][:, c * THIRD + t:(c + 1) * THIRD + t],
                                            start=t == 0, stop=t == TAPS - 1)
                    ins.then_inc(s["conv_summed"], 1)
                for k in range(2):
                    pe.wait_ge(s["xconv_ready"], n[k])
                    product(k, chip.dt_w[:, :], xconv[k], rows=S).then_inc(s["dt_ready"], 1)
                for k in range(2):
                    pe.wait_ge(s["decay_ready"], n[k])
                    product(k, chip.b_w[:, :], xconv[k], rows=S).then_inc(s["b_ready"], 1)
                for k in range(2):
                    pe.wait_ge(s["y_ready"], n[k])
                    product(k, chip.c_w[:, :], y[k], contracted=S).then_inc(s["c_ready"], 1)
                for k in range(2):
                    pe.wait_ge(s["g_ready"], n[k])
                    product(k, chip.out_w[:, :], g[k]).then_inc(s["out_ready"], 1)

def normalize(nc, chip, dram, images):
    turns = images // 4
    with ExitStack() as ctx:
        def sem(name):
            return ctx.enter_context(nc.semaphore(name))

        def two(name):
            return [ctx.enter_context(nc.sbuf_tensor(f"{name}{k}", [P, TP], F32)) for k in range(2)]

        def small(name, cols):
            return ctx.enter_context(nc.sbuf_tensor(name, [P, cols], F32))

        mixed, h_in, h, xc, sq, rstd, inv, ms, z, hn = (
            two("n_" + x) for x in ("mixed", "h_in", "h", "xc", "sq", "rstd", "inv", "ms", "z", "hn"))
        own, both, spread, var = small("own", 2), small("both", 1), small("spread", 1), small("var", 1)

        loaded = [sem("n_loaded0"), sem("n_loaded1")]
        stored = [sem("n_stored0"), sem("n_stored1")]
        tail_stored = sem("tail_stored")
        batch = sem("batch")
        batch_summed = sem("batch_summed")
        batch_power = sem("batch_power")
        names = """scaled_ready h_ready mean_ready xc_ready sq_ready var_ready log_ready rstd_ready inv_ready
            ms_ready log2_ready rms_ready z_ready hn_ready""".split()
        s = {name: sem("n_" + name) for name in names}
        bank = chip.bank

        block = ctx.enter_context(nc.Block())

        def rows(name, image):
            return bass.AP(dram[name].tensor, image * (D * TP), [[TP, P], [1, TP]])

        @block.sync
        def _(sp):
            def load(i, k):
                sp.dma_start(h_in[k][:, :], rows("h", 4 * i + 2 * k)).then_inc(loaded[k], 16)
                sp.dma_start(mixed[k][:, :], rows("mixed", 4 * i + 2 * k)).then_inc(loaded[k], 16)

            def store(i):
                for ready, tile, to in (("h_ready", h, "h2"), ("z_ready", z, "z"), ("hn_ready", hn, "hn")):
                    for k in range(2):
                        sp.wait_ge(s[ready], 2 * i + k + 1)
                        sp.dma_start(rows(to, 4 * i + 2 * k), tile[k][:, :]).then_inc(stored[k], 16)

            for k in range(2):
                load(0, k)
            if turns > 1:
                with sp.Fori(0, turns - 1) as i:
                    for k in range(2):
                        sp.wait_ge(s["h_ready"], 2 * i + k + 1)
                        load(i + 1, k)
                    store(i)
            store(turns - 1)
            for n in range(AHEAD):
                sp.dma_start(bass.AP(dram["hn"].tensor, (images + n) * D * TP, [[TP, D], [1, TP]]),
                             hn[0][0:D, :]).then_inc(tail_stored, 16)
            sp.dma_start(bass.AP(dram["z"].tensor, images * D * TP, [[TP, D], [1, TP]]),
                         hn[0][0:D, :]).then_inc(tail_stored, 16)
            for name in ("h2", "x2"):
                sp.dma_start(rows(name, images), hn[0][:, :]).then_inc(tail_stored, 16)
            sp.wait_ge(tail_stored, 16 * (AHEAD + 3))
            for k in range(2):
                sp.wait_ge(stored[k], 48 * turns)

        @block.tensor
        def _(pe):
            pe.wait_ge(batch, 1)
            pe.matmul(bank[6][:, 0:2], chip.const(C_HALF), own[:, :], start=True, stop=True).then_inc(batch_summed, 1)
            pe.wait_ge(batch, 4)
            pe.matmul(bank[6][:, 0:1], chip.const(C_HALF), spread[:, :], start=True, stop=True)\
              .then_inc(batch_summed, 1)

            def average(k, x):
                for c in range(3):
                    ins = pe.matmul(bank[3 * k + c][:, 0:THIRD], chip.const(C_MEAN),
                                    x[:, c * THIRD:(c + 1) * THIRD], start=True, stop=True)
                return ins

            with pe.Fori(0, turns) as i:
                n = [pe.snap(2 * i + k + 1) for k in range(2)]
                for k in range(2):
                    pe.wait_ge(s["h_ready"], n[k])
                    pe.wait_ge(s["ms_ready"], 2 * i)
                    average(k, h[k]).then_inc(s["mean_ready"], 1)
                for k in range(2):
                    pe.wait_ge(s["sq_ready"], n[k])
                    average(k, sq[k]).then_inc(s["var_ready"], 1)

        @block.scalar
        def _(act):
            act.wait_ge(batch, 5)
            act.activation(var[:, :], var[:, :], ACT.Ln).then_inc(batch_power, 1)
            act.wait_ge(batch_power, 1)
            act.activation(var[:, :], var[:, :], ACT.Exp, scale=-0.5).then_inc(batch_power, 1)
            act.wait_ge(batch, 8)
            with act.Fori(0, turns) as i:
                n = [act.snap(2 * i + k + 1) for k in range(2)]
                for k in range(2):
                    act.wait_ge(loaded[k], (i + 1) * 32)
                    act.wait_ge(s["h_ready"], 2 * i)
                    act.activation(mixed[k][:, :], mixed[k][:, :], ACT.Identity, scale=chip.v("bn_a"),
                                   bias=chip.v("bn_b")).then_inc(s["scaled_ready"], 1)
                for k in range(2):
                    act.wait_ge(s["xc_ready"], n[k])
                    act.activation(sq[k][:, :], xc[k][:, :], ACT.Square).then_inc(s["sq_ready"], 1)
                for k in range(2):
                    act.wait_ge(s["var_ready"], n[k])
                    act.activation(thirds(rstd[k][:, :]), chip.thirds(3 * k), ACT.Ln,
                                   bias=chip.v("ln_eps")).then_inc(s["log_ready"], 1)
                for k in range(2):
                    act.wait_ge(s["log_ready"], n[k])
                    act.activation(inv[k][:, :], rstd[k][:, :], ACT.Exp, scale=-1.0).then_inc(s["inv_ready"], 1)
                for k in range(2):
                    act.wait_ge(s["inv_ready"], n[k])
                    act.activation(rstd[k][:, :], rstd[k][:, :], ACT.Exp, scale=-0.5).then_inc(s["rstd_ready"], 1)
                for k in range(2):
                    act.wait_ge(s["ms_ready"], n[k])
                    act.activation(ms[k][:, :], ms[k][:, :], ACT.Ln, bias=chip.v("rms_eps"))\
                       .then_inc(s["log2_ready"], 1)
                for k in range(2):
                    act.wait_ge(s["log2_ready"], n[k])
                    act.activation(ms[k][:, :], ms[k][:, :], ACT.Exp, scale=-0.5).then_inc(s["rms_ready"], 1)

        @block.vector
        def _(dve):
            dve.bn_aggr(own[:, :], chip.stats[:, :].rearrange("p (n s) -> p n s", s=6)).then_inc(batch, 1)
            dve.wait_ge(batch_summed, 1)
            dve.tensor_copy(both[:, :], bank[6][:, 0:1]).then_inc(batch, 1)
            dve.wait_ge(batch, 2)
            dve.tensor_tensor(spread[:, :], own[:, 0:1], both[:, :], ALU.subtract).then_inc(batch, 1)
            dve.wait_ge(batch, 3)
            dve.scalar_tensor_tensor(spread[:, :], spread[:, :], spread[:, 0:1], own[:, 1:2], ALU.mult, ALU.add)\
               .then_inc(batch, 1)
            dve.wait_ge(batch_summed, 2)
            dve.tensor_scalar(var[:, :], bank[6][:, 0:1], BN_EPS, None, ALU.add).then_inc(batch, 1)
            dve.wait_ge(batch_power, 2)
            dve.tensor_tensor(chip.v("bn_a"), var[:, :], chip.v("gamma"), ALU.mult).then_inc(batch, 1)
            dve.wait_ge(batch, 6)
            dve.tensor_tensor(both[:, :], both[:, :], chip.v("bn_a"), ALU.mult).then_inc(batch, 1)
            dve.wait_ge(batch, 7)
            dve.tensor_tensor(chip.v("bn_b"), chip.v("beta"), both[:, :], ALU.subtract).then_inc(batch, 1)
            with dve.Fori(0, turns) as i:
                n = [dve.snap(2 * i + k + 1) for k in range(2)]
                for k in range(2):
                    dve.wait_ge(s["scaled_ready"], n[k])
                    dve.wait_ge(stored[k], 48 * i)
                    dve.tensor_tensor(h[k][:, :], h_in[k][:, :], mixed[k][:, :], ALU.add).then_inc(s["h_ready"], 1)
                for k in range(2):
                    dve.wait_ge(s["mean_ready"], n[k])
                    dve.tensor_tensor(thirds(xc[k][:, :]), thirds(h[k][:, :]), chip.thirds(3 * k), ALU.subtract)\
                       .then_inc(s["xc_ready"], 1)
                for k in range(2):
                    dve.wait_ge(s["inv_ready"], n[k])
                    dve.tensor_tensor(thirds(ms[k][:, :]), chip.thirds(3 * k), thirds(inv[k][:, :]), ALU.mult)\
                       .then_inc(s["ms_ready"], 1)
                for k in range(2):
                    dve.wait_ge(s["rstd_ready"], n[k])
                    dve.tensor_tensor(z[k][:, :], xc[k][:, :], rstd[k][:, :], ALU.mult).then_inc(s["z_ready"], 1)
                for k in range(2):
                    dve.wait_ge(s["rms_ready"], n[k])
                    dve.wait_ge(s["z_ready"], n[k])
                    dve.tensor_tensor(hn[k][:, :], z[k][:, :], ms[k][:, :], ALU.mult).then_inc(s["hn_ready"], 1)



HI, MID, LO = range(3)
Q_TERMS = (HI, HI, MID, HI, LO, MID)
K_TERMS = (HI, MID, HI, LO, HI, MID)
TERMS = len(Q_TERMS)
SPLIT = TERMS * HD
BIASED = SPLIT + 3

M_COLS = TILES * NH + 1


def max_items():
    items = []
    for tile in range(TILES):
        keys = P * (tile + 1)
        for part, first, n in ((0, 0, min(keys, 512)), (1, 512, keys - 512)):
            if n > 0:
                heads = {P: 4, 2 * P: 2}.get(n, 1)
                items += [(tile, h, heads, first, n, part) for h in range(0, NH, heads)]
    return items + [(TILES, 0, NH, 0, 512, 0), (TILES, 0, NH, 512, 512, 1), (TILES, 0, NH, 1024, 1, 2)]


Q_CHUNKS = ((0, 384), (384, 768), (768, TP))


def prob_sets():
    return [(c, j, max(lo, P * j), hi - max(lo, P * j))
            for c, (lo, hi) in enumerate(Q_CHUNKS) for j in range(9) if P * j < hi]


MAX_ITEMS = max_items()
SETS = prob_sets()
N_MAX, N_SETS = len(MAX_ITEMS), len(SETS)
LAST_SET = [max(t for t, x in enumerate(SETS) if x[0] == c) for c in range(3)]
RING = 6


def attention_order():
    order, maxima, later, turns = [], 0, [], 0
    for t in range(N_SETS):
        step = later.pop(0) if later else []
        order += step + [("scores", t)]
        until = min(N_MAX, -(-N_MAX * (t + 1) // (N_SETS - 2)))
        if t:
            order.append(("values", t - 1))
            if t - 1 in LAST_SET:
                c = LAST_SET.index(t - 1)
                order.append(("gather", c))
                later = [[("denominators", c)], [], [("output", c)]]
        items = [("max", q) for q in range(maxima, until)]
        order += items[:1]
        if not step and t >= 3 and turns < 6:
            order.append(("turn", turns))
            turns += 1
        order += items[1:]
        if maxima < N_MAX == until:
            order.append(("shift", 0))
        elif maxima == N_MAX and ("shift_rows", 0) not in order:
            order.append(("shift_rows", 0))
        maxima = until
    for x in later:
        order += x
    left = [("turn", c) for c in range(turns, 6)]
    return order + ([("values", N_SETS - 1), ("gather", 2), ("project_v", 0)] + left[:1] + [("denominators", 2)]
                    + left[1:-1] + [("output", 2)] + (left[1:] and left[-1:]))


ORDER = attention_order()
SHARED_KINDS = ("turn", "project_v", "shift_rows", "denominators", "output")
SHARED = [x for x in ORDER if x[0] in SHARED_KINDS]
PROLOGUE_SHARED = 2 * (6 + 1) + 6 + 1


class Image:

    def __init__(self, i, offset):
        self.slot = offset % 2
        self.number = 2 * i + offset
        self.i, self.earlier = i, offset // 2

    def times(self, n, more=0):
        return self.number * n + more

    def of_slot(self, n, more=0):
        return self.i * n + (self.earlier * n + more)


FIRST_IMAGE = Image(0, 0)


def attend(nc, chip, dram, images):
    bank, psum = chip.bank, chip.psum
    dram["parts"] = nc.dram_tensor("scratch_parts", [2, QK, 3, TP], BF16, kind="Internal").ap()
    dram["shift"] = nc.dram_tensor("scratch_shift", [2, 3 * M_COLS, P], BF16, kind="Internal").ap()
    with ExitStack() as ctx:
        def sem(name):
            return ctx.enter_context(nc.semaphore("a_" + name))

        def sb(name, cols, dt=F32):
            return ctx.enter_context(nc.sbuf_tensor("a_" + name, [P, cols], dt))

        hn = [sb(f"hn{k}", TP) for k in range(2)]
        z = [sb(f"z{k}", TP) for k in range(2)]
        by_cos, by_sin, qk = sb("by_cos", TP), sb("by_sin", TP), sb("qk", TP)
        rest = sb("rest", TP)
        parts = sb("parts", 3 * TP, BF16)
        flat = [sb(f"split{k}", (NH + NKV) * TP, BF16) for k in range(2)]
        flat_b = [sb(f"biased{k}", (NH + NKV) * TP, BF16) for k in range(2)]
        split = [x[:, :].rearrange("p (h n) -> p h n", h=NH + NKV) for x in flat]
        biased = [x[:, :].rearrange("p (h n) -> p h n", h=NH + NKV) for x in flat_b]
        values = [sb(f"values{k}", 9 * NKV * 32) for k in range(2)]
        v = [x[:, :].rearrange("p (t g c) -> p t g c", t=9, g=NKV) for x in values]
        probs = [sb(f"probs{r}", 2 * 384) for r in range(RING)]
        pr = [x[:, :].rearrange("p (h n) -> p h n", h=2) for x in probs]
        maxima = sb("maxima", 3 * M_COLS)
        mx = maxima[:, :].rearrange("p (a m) -> p a m", a=3)
        shift, shift_rest = sb("shift", M_COLS), sb("shift_rest", M_COLS)
        shift_parts = sb("shift_parts", 3 * M_COLS, BF16)
        sp3 = shift_parts[:, :].rearrange("p (a m) -> p a m", a=3)
        shift_row = sb("shift_row", P, BF16)
        unnormed, recip, y = sb("unnormed", 384), sb("recip", 384), sb("y", 384)
        x2 = sb("x2", TP)

        MAX_BANKS, SCORE_BANKS, SUM_BANK, SHARED_BANK = (0, 1), (2, 4), 6, 7
        shared, summed = bank[SHARED_BANK], bank[SUM_BANK]

        cleared = sem("cleared")
        hn_loaded = [sem(f"hn_loaded{k}") for k in range(2)]
        z_loaded = [sem(f"z_loaded{k}") for k in range(2)]
        shared_ready = sem("shared_ready")
        shared_read = sem("shared_read")
        split_steps = sem("split_steps")
        parts_stored = sem("parts_stored")
        split_loaded = [sem(f"split_loaded{k}") for k in range(2)]
        biased_loaded = [sem(f"biased_loaded{k}") for k in range(2)]
        shift_stored = sem("shift_stored")
        shift_placed = [sem(f"shift_placed{k}") for k in range(2)]
        max_scores = sem("max_scores")
        max_taken = sem("max_taken")
        shift_steps = sem("shift_steps")
        scores = sem("scores")
        exps = sem("exps")
        summed_sets = sem("summed_sets")
        unnormed_ready = sem("unnormed_ready")
        y_ready = sem("y_ready")
        x2_stored = sem("x2_stored")
        NSPLIT, NSHIFT, SHIFT_DMAS, N_CLEARED = 5, 5, 2 * 16, 11

        def use(image, step):
            return image.number * len(SHARED) + (PROLOGUE_SHARED + SHARED.index(step) + 1)

        block = ctx.enter_context(nc.Block())

        def turn_images(i, k):
            return Image(i, k), Image(i, k + 1), Image(i, k + 2), Image(i, k + 3)

        @block.sync
        def _(sp):
            def load_hn(m):
                sp.dma_start(hn[m.slot][0:D, :], bass.AP(dram["hn"].tensor, m.times(D * TP), [[TP, D], [1, TP]]))\
                  .then_inc(hn_loaded[m.slot], 16)

            def load_z(m):
                sp.dma_start(z[m.slot][0:D, :], bass.AP(dram["z"].tensor, m.times(D * TP), [[TP, D], [1, TP]]))\
                  .then_inc(z_loaded[m.slot], 16)

            def lay_out_split(m):
                sp.wait_ge(split_steps, m.times(NSPLIT, NSPLIT))
                at = m.slot * (QK * 3 * TP)
                parts_dram = dram["parts"]
                sp.dma_start(bass.AP(parts_dram.tensor, at, [[3 * TP, QK], [1, 3 * TP]]), parts[0:QK, :])\
                  .then_inc(parts_stored, 16)
                sp.wait_ge(parts_stored, m.times(16, 16))
                for t in range(TERMS):
                    rows = slice(HD * t, HD * (t + 1))
                    for first, n, term in ((0, NH, Q_TERMS[t]), (NH, NKV, K_TERMS[t])):
                        src = bass.AP(parts_dram.tensor, at + first * HD * 3 * TP + term * TP,
                                      [[3 * TP, HD], [HD * 3 * TP, n], [1, TP]])
                        sp.dma_start(split[m.slot][rows, first:first + n, :], src)\
                          .then_inc(split_loaded[m.slot], 16)

            def copy_biased(m):
                sp.wait_ge(split_loaded[m.slot], m.of_slot(16 * 2 * TERMS, 16 * 2 * TERMS))
                sp.dma_start(flat_b[m.slot][0:SPLIT, :], flat[m.slot][0:SPLIT, :])\
                  .then_inc(biased_loaded[m.slot], 16)

            def place_shift(m, taken):
                sp.wait_ge(shared_read, taken)
                rows_dram = dram["shift"].tensor
                at = m.slot * (3 * M_COLS * P)
                sp.dma_start(bass.AP(rows_dram, at, [[P, 3 * M_COLS], [1, P]]), shift_row[0:3 * M_COLS, :])\
                  .then_inc(shift_stored, 16)
                sp.wait_ge(shift_stored, m.times(16, 16))
                rows = slice(SPLIT, BIASED)
                sp.dma_start(biased[m.slot][rows, 0:NH, 0:L],
                             bass.AP(rows_dram, at, [[M_COLS * P, 3], [L, NH], [1, L]]))\
                  .then_inc(shift_placed[m.slot], 16)
                sp.dma_start(biased[m.slot][rows, 0:NH, L:TP],
                             bass.AP(rows_dram, at + NH * L + 30, [[M_COLS * P, 3], [32, NH], [1, 2]]))\
                  .then_inc(shift_placed[m.slot], 16)

            sp.wait_ge(cleared, N_CLEARED)
            first, second = Image(0, 0), Image(0, 1)
            load_hn(first)
            load_hn(second)
            load_z(first)
            sp.wait_ge(shared_ready, 7)
            load_hn(Image(0, 2))
            lay_out_split(first)
            copy_biased(first)
            lay_out_split(second)
            place_shift(first, PROLOGUE_SHARED)
            with sp.Fori(0, images // 2) as i:
                for k in range(2):
                    now, soon, later, last = turn_images(i, k)
                    sp.wait_ge(shared_read, now.times(len(SHARED), PROLOGUE_SHARED))
                    load_z(soon)
                    load_hn(last)
                    copy_biased(soon)
                    sp.wait_ge(max_scores, soon.times(N_MAX))
                    sp.wait_ge(biased_loaded[later.slot], later.of_slot(16))
                    lay_out_split(later)
                    place_shift(soon, use(now, ("shift_rows", 0)))
                    sp.wait_ge(shared_read, use(now, ("output", 2)))
                    sp.dma_start(bass.AP(dram["x2"].tensor, now.times(D * TP), [[TP, D], [1, TP]]), x2[0:D, :])\
                      .then_inc(x2_stored, 16)
            sp.wait_ge(x2_stored, 16 * images)
            for k in range(2):
                n = images // 2
                sp.wait_ge(hn_loaded[k], 16 * (n + 2 - k))
                sp.wait_ge(split_loaded[k], (n + 1) * (16 * 2 * TERMS))
                for fetched, by in ((z_loaded, 16), (biased_loaded, 16), (shift_placed, SHIFT_DMAS)):
                    sp.wait_ge(fetched[k], by * (n + 1 - k))

        @block.gpsimd
        def _(pool):
            for k in range(2):
                pool.memset(values[k][:, 0:TILES * NKV * 32], 1.0).then_inc(cleared, 1)
                pool.memset(values[k][:, TILES * NKV * 32:], 0.0).then_inc(cleared, 1)
            pool.memset(maxima[:, :], -3e38).then_inc(cleared, 1)
            pool.wait_ge(cleared, N_CLEARED - 2)
            for k in range(2):
                pool.memset(values[k][0:1, TILES * NKV * 32:], 1.0).then_inc(cleared, 1)
            pool.wait_ge(cleared, N_CLEARED)

            def split_up(m, turned):
                p3 = parts[0:QK, :].rearrange("p (a n) -> p a n", a=3)
                step = m.times(NSPLIT)
                pool.wait_ge(shared_read, turned)
                pool.tensor_tensor(qk[0:QK, :], by_cos[0:QK, :], by_sin[0:QK, :], ALU.add).then_inc(split_steps, 1)
                pool.wait_ge(parts_stored, m.times(16))
                pool.tensor_tensor(p3[:, HI, :], by_cos[0:QK, :], by_sin[0:QK, :], ALU.add).then_inc(split_steps, 1)
                pool.wait_ge(split_steps, step + 2)
                pool.tensor_tensor(rest[0:QK, :], qk[0:QK, :], p3[:, HI, :], ALU.subtract).then_inc(split_steps, 1)
                pool.tensor_tensor(p3[:, MID, :], qk[0:QK, :], p3[:, HI, :], ALU.subtract).then_inc(split_steps, 1)
                pool.wait_ge(split_steps, step + 4)
                pool.tensor_tensor(p3[:, LO, :], rest[0:QK, :], p3[:, MID, :], ALU.subtract).then_inc(split_steps, 1)

            split_up(Image(0, 0), 6)
            split_up(Image(0, 1), 13)
            with pool.Fori(0, images // 2) as i:
                for k in range(2):
                    now, _, later, _ = turn_images(i, k)
                    split_up(later, now.times(len(SHARED), PROLOGUE_SHARED))

        @block.scalar
        def _(act):
            act.wait_ge(cleared, N_CLEARED)

            def take_v(m, at):
                act.wait_ge(shared_ready, at)
                got = shared[:, 0:9 * NKV * HD].rearrange("p (t g c) -> p t g c", t=9, g=NKV)
                act.activation(v[m.slot][:, 0:8, :, 0:HD].rearrange("p t g c -> p (t g) c"),
                               got[:, 0:8].rearrange("p t g c -> p (t g) c"), ACT.Copy)
                act.activation(v[m.slot][0:1, 8, :, 0:HD], got[0:1, 8], ACT.Copy).then_inc(shared_read, 1)

            def take_row(m, at):
                act.wait_ge(shared_ready, at)
                act.activation(shift_row[0:3 * M_COLS, :], shared[:, :].bitcast(BF16)[0:3 * M_COLS, 0:P], ACT.Copy)\
                   .then_inc(shared_read, 1)

            take_v(Image(0, 0), 7)
            take_v(Image(0, 1), 14)
            take_row(Image(0, 0), PROLOGUE_SHARED)
            with act.Fori(0, images // 2) as i:
                for k in range(2):
                    now, soon, later, _ = turn_images(i, k)
                    for kind, x in ORDER:
                        if kind == "scores":
                            c, j, first, n = SETS[x]
                            keys = P if j < TILES else 1
                            act.wait_ge(summed_sets, now.times(N_SETS, max(x - RING // 2 + 1, 0)))
                            for half in range(2):
                                act.wait_ge(scores, now.times(2 * N_SETS, 2 * x + half + 1))
                                b = SCORE_BANKS[half]
                                act.activation(pr[(2 * x + half) % RING][0:keys, :, 0:n],
                                               psum[0:keys, b:b + 2, 0:n], ACT.Exp, scale=HD ** -0.5)\
                                   .then_inc(exps, 1)
                        elif kind == "gather":
                            w = Q_CHUNKS[x][1] - Q_CHUNKS[x][0]
                            act.wait_ge(summed_sets, now.times(N_SETS, LAST_SET[x] + 1))
                            act.wait_ge(y_ready, now.times(3, x))
                            act.activation(unnormed[:, 0:w], summed[:, 0:w], ACT.Copy).then_inc(unnormed_ready, 1)
                        elif kind == "project_v":
                            act.wait_ge(summed_sets, now.times(N_SETS, N_SETS))
                            take_v(later, use(now, (kind, x)))
                        elif kind == "shift_rows":
                            act.wait_ge(shift_placed[now.slot], now.of_slot(SHIFT_DMAS, SHIFT_DMAS))
                            take_row(soon, use(now, (kind, x)))

        @block.vector
        def _(dve):
            for k in range(2):
                dve.memset(hn[k][D:P, :], 0.0).then_inc(cleared, 1)
                dve.memset(flat_b[k][SPLIT:P, NH * TP:], 1.0).then_inc(cleared, 1)
            dve.wait_ge(cleared, N_CLEARED)

            def take_turn(m, c, at):
                third, swapped = divmod(c, 2)
                to, table = (by_sin, C_SIN) if swapped else (by_cos, C_COS)
                cols = slice(third * THIRD, (third + 1) * THIRD)
                dve.wait_ge(shared_ready, at)
                dve.tensor_tensor(to[0:QK, cols], shared[0:QK, 0:THIRD], chip.const(table, TP)[0:QK, cols], ALU.mult)\
                   .then_inc(shared_read, 1)

            def take_max(m, q):
                tile, h, heads, _, n, part = MAX_ITEMS[q]
                dve.wait_ge(max_scores, m.times(N_MAX, q + 1))
                b = MAX_BANKS[(m.slot * N_MAX + q) % 2]
                if tile < TILES:
                    got = bank[b][:, 0:heads * n].rearrange("p (h n) -> p h n", h=heads)
                    col = h * TILES + tile
                    to = mx[:, part, col:col + (heads - 1) * TILES + 1:TILES]
                else:
                    got, to = bank[b][:, 0:n], mx[:, part, M_COLS - 1:M_COLS]
                dve.tensor_reduce(to, got, AX_X, ALU.max).then_inc(max_taken, 1)

            def split_shift(m):
                step = m.times(NSHIFT)
                dve.wait_ge(max_taken, m.times(N_MAX, N_MAX))
                dve.tensor_reduce(shift[:, :], mx.rearrange("p a m -> p m a"), AX_X, ALU.max)\
                   .then_inc(shift_steps, 1)
                dve.wait_ge(shift_steps, step + 1)
                dve.tensor_scalar(sp3[:, HI, :], shift[:, :], -1.0, None, ALU.mult).then_inc(shift_steps, 1)
                dve.wait_ge(shift_steps, step + 2)
                dve.scalar_tensor_tensor(shift_rest[:, :], shift[:, :], -1.0, sp3[:, HI, :], ALU.mult, ALU.subtract)\
                   .then_inc(shift_steps, 1)
                dve.wait_ge(shift_steps, step + 3)
                dve.tensor_copy(sp3[:, MID, :], shift_rest[:, :]).then_inc(shift_steps, 1)
                dve.wait_ge(shift_steps, step + 4)
                dve.tensor_tensor(sp3[:, LO, :], shift_rest[:, :], sp3[:, MID, :], ALU.subtract)\
                   .then_inc(shift_steps, 1)

            for n in range(3):
                for c in range(6):
                    if n > 0 and c == 0:
                        dve.wait_ge(split_steps, (n - 1) * NSPLIT + 2)
                    take_turn(Image(0, n), c, n * 7 + c + 1)
            for q in range(N_MAX):
                take_max(Image(0, 0), q)
            split_shift(Image(0, 0))
            with dve.Fori(0, images // 2) as i:
                for k in range(2):
                    now, soon, later, last = turn_images(i, k)
                    for kind, x in ORDER:
                        if kind == "turn":
                            if x == 0:
                                dve.wait_ge(split_steps, later.times(NSPLIT, 2))
                            take_turn(last, x, use(now, (kind, x)))
                        elif kind == "max":
                            take_max(soon, x)
                        elif kind == "shift":
                            split_shift(soon)
                        elif kind == "denominators":
                            w = Q_CHUNKS[x][1] - Q_CHUNKS[x][0]
                            dve.wait_ge(shared_ready, use(now, (kind, x)))
                            dve.wait_ge(y_ready, now.times(3, x))
                            dve.reciprocal(recip[:, 0:w], shared[:, 0:w]).then_inc(shared_read, 1)
                            dve.wait_ge(shared_read, use(now, (kind, x)))
                            dve.wait_ge(unnormed_ready, now.times(3, x + 1))
                            dve.tensor_tensor(y[:, 0:w], unnormed[:, 0:w], recip[:, 0:w], ALU.mult)\
                               .then_inc(y_ready, 1)
                        elif kind == "output":
                            lo, hi = Q_CHUNKS[x]
                            dve.wait_ge(shared_ready, use(now, (kind, x)))
                            if x == 0:
                                dve.wait_ge(z_loaded[now.slot], now.of_slot(16, 16))
                                dve.wait_ge(x2_stored, now.times(16))
                            dve.tensor_tensor(x2[0:D, lo:hi], z[now.slot][0:D, lo:hi], shared[0:D, 0:hi - lo], ALU.add)\
                               .then_inc(shared_read, 1)

        @block.tensor
        def _(pe):
            pe.wait_ge(cleared, N_CLEARED)

            def turn(m, c, at):
                third, swapped = divmod(c, 2)
                if c == 0:
                    pe.wait_ge(hn_loaded[m.slot], m.of_slot(16, 16))
                pe.wait_ge(shared_read, at - 1)
                pe.matmul(shared[0:QK, 0:THIRD], (chip.qk_swapped if swapped else chip.qk_w)[:, :],
                          hn[m.slot][:, third * THIRD:(third + 1) * THIRD], start=True, stop=True)\
                  .then_inc(shared_ready, 1)

            def project_v(m, at):
                pe.wait_ge(shared_read, at - 1)
                n = NKV * HD
                for t in range(9):
                    keys = P if t < TILES else 2
                    ins = pe.matmul(shared[0:keys, t * n:(t + 1) * n], hn[m.slot][:, t * P:t * P + keys],
                                    chip.v_w[:, :], start=True, stop=True)
                ins.then_inc(shared_ready, 1)

            def score_for_max(m, q):
                tile, h, heads, first, n, _ = MAX_ITEMS[q]
                x = split[m.slot]
                if q == 0:
                    pe.wait_ge(split_loaded[m.slot], m.of_slot(16 * 2 * TERMS, 16 * 2 * TERMS))
                if m is not FIRST_IMAGE or q >= 2:
                    pe.wait_ge(max_taken, m.times(N_MAX, q - 1))
                b = MAX_BANKS[(m.slot * N_MAX + q) % 2]
                if tile == TILES:
                    for a in range(NH):
                        ins = pe.matmul(bank[b][32 * a:32 * (a + 1), 0:n], x[0:SPLIT, a, TP - 32:TP],
                                        x[0:SPLIT, NH + a // 2, first:first + n], start=True, stop=True)
                else:
                    diagonal = first + n == P * (tile + 1)
                    for a in range(heads):
                        ins = pe.matmul(bank[b][:, a * n:(a + 1) * n], x[0:SPLIT, h + a, P * tile:P * (tile + 1)],
                                        x[0:SPLIT, NH + (h + a) // 2, first:first + n],
                                        start=True, stop=not diagonal)
                        if diagonal:
                            ins = pe.matmul(bank[b][:, (a + 1) * n - P:(a + 1) * n], chip.ident16[:, :],
                                            chip.mask_q16[:, :], start=False, stop=True)
                ins.then_inc(max_scores, 1)

            def turn_shift(m, at):
                pe.wait_ge(shift_steps, m.times(NSHIFT, NSHIFT))
                pe.wait_ge(shared_read, at - 1)
                pe.transpose(shared[:, :].bitcast(BF16)[0:3 * M_COLS, 0:P], shift_parts[:, :], chip.ident16[:, :])\
                  .then_inc(shared_ready, 1)

            def score(m, t):
                c, j, first, n = SETS[t]
                keys = P if j < TILES else 1
                x = biased[m.slot]
                if t == 0:
                    pe.wait_ge(biased_loaded[m.slot], m.of_slot(16, 16))
                    pe.wait_ge(shift_placed[m.slot], m.of_slot(SHIFT_DMAS, SHIFT_DMAS))
                masked = P * j >= Q_CHUNKS[c][0] and j < TILES
                for half in range(2):
                    pe.wait_ge(exps, m.times(2 * N_SETS, max(2 * t + half - 1, 0)))
                    for a in range(2):
                        b = SCORE_BANKS[half] + a
                        ins = pe.matmul(bank[b][0:keys, 0:n], x[0:BIASED, NH + half, P * j:P * j + keys],
                                        x[0:BIASED, 2 * half + a, first:first + n], start=True, stop=not masked)
                        if masked:
                            ins = pe.matmul(bank[b][:, 0:P], chip.ident16[:, :], chip.mask_k16[:, :],
                                            start=False, stop=True)
                    ins.then_inc(scores, 1)

            def weigh_values(m, t):
                c, j, first, n = SETS[t]
                lo, hi = Q_CHUNKS[c]
                if j == 0:
                    pe.wait_ge(unnormed_ready, m.times(3, c))
                last = t in LAST_SET
                for h in range(NH):
                    if h % 2 == 0:
                        pe.wait_ge(exps, m.times(2 * N_SETS, 2 * t + h // 2 + 1))
                    ins = pe.matmul(summed[32 * h:32 * (h + 1), first - lo:hi - lo],
                                    v[m.slot][:, j, h // 2, :],
                                    pr[(2 * t + h // 2) % RING][:, h % 2, 0:n], start=j == 0, stop=last)
                ins.then_inc(summed_sets, 1)

            for n in range(3):
                for c in range(6):
                    turn(Image(0, n), c, n * 7 + c + 1)
                if n < 2:
                    project_v(Image(0, n), n * 7 + 7)
            for q in range(N_MAX):
                score_for_max(FIRST_IMAGE, q)
            turn_shift(Image(0, 0), PROLOGUE_SHARED)
            with pe.Fori(0, images // 2) as i:
                for k in range(2):
                    now, soon, later, last = turn_images(i, k)
                    for kind, x in ORDER:
                        at = use(now, (kind, x)) if kind in SHARED_KINDS else None
                        if kind == "scores":
                            score(now, x)
                        elif kind == "values":
                            weigh_values(now, x)
                        elif kind == "max":
                            score_for_max(soon, x)
                        elif kind == "turn":
                            turn(last, x, at)
                        elif kind == "project_v":
                            project_v(later, at)
                        elif kind == "shift_rows":
                            turn_shift(soon, at)
                        elif kind == "denominators":
                            w = Q_CHUNKS[x][1] - Q_CHUNKS[x][0]
                            pe.wait_ge(unnormed_ready, now.times(3, x + 1))
                            pe.wait_ge(shared_read, at - 1)
                            pe.matmul(shared[:, 0:w], chip.const(C_DEN), unnormed[:, 0:w], start=True, stop=True)\
                              .then_inc(shared_ready, 1)
                        elif kind == "output":
                            w = Q_CHUNKS[x][1] - Q_CHUNKS[x][0]
                            pe.wait_ge(y_ready, now.times(3, x + 1))
                            pe.wait_ge(shared_read, at - 1)
                            pe.matmul(shared[0:D, 0:w], chip.o_w[:, :], y[:, 0:w], start=True, stop=True)\
                              .then_inc(shared_ready, 1)



UNITS = 3 * 2 * PAIRS * 3
GROUPS = UNITS // 3
LAG = 2
G_THIRD = 2 * PAIRS
EMIT_TILES = (range(0, 2), range(2, 5), range(5, 9))
HIDDEN_RING = 4


CHOICES = 13
CHOSEN = 2 * CHOICES - 1


def experts_order():
    ahead = {3: ("square", 0), 5: ("mean", 0), 6: ("mean", 1), 7: ("mean", 2), 8: ("norm", 0), 10: ("split", 0),
             12: ("split", 1), 13: ("route", 0), 34: ("turn_weights", 0), 36: ("turn_weights", 1)}
    order = []
    for u in range(UNITS + LAG):
        if u < UNITS:
            if u % 3 == 0:
                order.append(("spread", u // 3))
            order.append(("up", u))
        if u >= LAG:
            order.append(("down", u - LAG))
            if (u - LAG) % 3 == 2:
                order.append(("weigh", (u - LAG) // 3))
        if u >= LAG + 1 and (u - LAG - 1) % 3 == 2:
            g = (u - LAG - 1) // 3
            order.append(("fold", g))
            if g % G_THIRD == G_THIRD - 1:
                order += [("close", g // G_THIRD), ("emit", g // G_THIRD)]
        if u in ahead:
            order.append(ahead[u])
        if u == 13:
            order += [("choose", 0), ("exponents", 0)]
        elif 17 <= u < 17 + CHOICES - 1:
            order.append(("choose", u - 16))
    g = GROUPS - 1
    return order + [("fold", g), ("close", g // G_THIRD), ("emit", g // G_THIRD)]


E_ORDER = experts_order()
E_SHARED_KINDS = ("spread", "mean", "route", "turn_weights", "emit")
E_SHARED = [x for x in E_ORDER if x[0] in E_SHARED_KINDS]
E_PROLOGUE = [("square", 0), ("mean", 0), ("mean", 1), ("mean", 2), ("norm", 0), ("split", 0),
              ("split", 1), ("route", 0), ("choose", 0), ("exponents", 0)]
E_PROLOGUE += [("choose", x) for x in range(1, CHOICES)]
E_PROLOGUE += [("turn_weights", 0), ("turn_weights", 1)]
E_PROLOGUE_SHARED = [x for x in E_PROLOGUE if x[0] in E_SHARED_KINDS]


def route_and_mix_experts(nc, chip, dram, images):
    bank = chip.bank
    turns = images // 4
    A_BANKS, B_BANKS, OUT_BANKS, SUM_BANK, SHARED_BANK = (0, 1), (2, 3), (4, 5), 6, 7
    shared, total = bank[SHARED_BANK], bank[SUM_BANK]
    GR = 9 * 2
    with ExitStack() as ctx:
        def sem(name):
            return ctx.enter_context(nc.semaphore("e_" + name))

        def sb(name, cols, dt=F32):
            return ctx.enter_context(nc.sbuf_tensor("e_" + name, [P, cols], dt))

        x2 = [sb(f"x2{k}", TP) for k in range(2)]
        h2 = [sb(f"h2{k}", TP) for k in range(2)]
        base = [sb(f"base{k}", TP) for k in range(2)]
        flat = sb("flat", TP)
        high, low = sb("high", TP, F16), sb("low", TP, F16)
        halves = [[sb(f"halves{k}{b}", TP, F16) for b in range(2)] for k in range(2)]
        turned = [sb(f"turned{k}", 9 * P, BF16) for k in range(2)]
        squares, rms = sb("squares", TP), sb("rms", TP)
        gate = [sb(f"gate{r}", THIRD) for r in range(HIDDEN_RING)]
        hidden = [sb(f"hidden{r}", THIRD) for r in range(HIDDEN_RING)]
        spread = [sb(f"spread{r}", THIRD) for r in range(2)]
        weighed = [sb(f"weighed{r}", THIRD) for r in range(2)]
        whole = sb("whole", TP)
        outs = [sb(f"outs{r}", 4 * P) for r in range(2)]
        logit, prob, one_hot, second, other = (sb(n, GR * NE) for n in ("logit", "prob", "one_hot", "second", "other"))
        best, best2, per_group = sb("best", GR), sb("best2", GR), sb("per_group", GR)
        wparts = sb("wparts", 9 * 96, BF16)

        cleared = sem("cleared")
        loaded = [sem(f"loaded{k}") for k in range(2)]
        stored = [sem(f"stored{k}") for k in range(2)]
        shared_ready, shared_read = sem("shared_ready"), sem("shared_read")
        squared = sem("squared")
        based = sem("based")
        rms_ready = sem("rms_ready")
        flat_ready = sem("flat_ready")
        moved = sem("moved")
        chosen = sem("chosen")
        exp_ready = sem("exp_ready")
        up_a, up_b = sem("up_a"), sem("up_b")
        gates, hiddens = sem("gates"), sem("hiddens")
        downs = sem("downs")
        weighs, folds, closes = sem("weighs"), sem("folds"), sem("closes")

        def use(n, step):
            return n * len(E_SHARED) + (len(E_PROLOGUE_SHARED) + E_SHARED.index(step) + 1)

        def use_first(step):
            return E_PROLOGUE_SHARED.index(step) + 1

        def rows(name, pair):
            return bass.AP(dram[name].tensor, pair * (2 * D * TP), [[TP, P], [1, TP]])

        def groups(ap):
            return ap[:, :].rearrange("p (g e) -> p g e", e=NE)

        def to_all(ap):
            return bass.AP(ap, 0, [[GR, P], [1, GR], [0, NE]])

        def third(ap, c):
            return ap[:, c * THIRD:(c + 1) * THIRD]

        def unit(u):
            return u // (2 * PAIRS * 3), u // (PAIRS * 3) % 2, u // 3 % PAIRS, u % 3

        EMITTED = [sum((2 + (x == 2)) for s in range(2) for x in range(3) if (s + x) % 2 == k) for k in range(2)]

        def emitted_before(i, k, x):
            r = (k + x) % 2
            inside = sum((2 + (xx == 2)) for s in range(2) for xx in range(3)
                         if (s + xx) % 2 == r and (s, xx) < (k, x))
            return i * (16 * EMITTED[r]) + 16 * inside

        block = ctx.enter_context(nc.Block())

        @block.sync
        def _(sp):
            def load(n, slot):
                sp.dma_start(x2[slot][:, :], rows("x2", n)).then_inc(loaded[slot], 16)
                sp.dma_start(h2[slot][:, :], rows("h2", n)).then_inc(loaded[slot], 16)

            def emit(n, slot, x):
                sp.wait_ge(shared_read, use(n, ("emit", x)))
                tiles = [t for t in EMIT_TILES[x] if t < TILES]
                r = outs[(slot + x) % 2]
                for b in range(2):
                    src = r[:, 0:len(tiles) * P].rearrange("p (t u d) -> p t u d", u=2, d=D)[:, :, b, :]
                    to = bass.AP(dram["out"].tensor, (2 * n + b) * (T * D) + tiles[0] * P * D,
                                 [[D, P], [P * D, len(tiles)], [1, D]])
                    sp.dma_start(to, src).then_inc(stored[(slot + x) % 2], 16)
                if x == 2:
                    sp.dma_start(bass.AP(dram["out"].tensor, 2 * n * (T * D) + L * D, [[0, 1], [T * D, 2], [1, D]]),
                                 r[0:1, 3 * P:4 * P].rearrange("p (u d) -> p u d", u=2))\
                      .then_inc(stored[(slot + x) % 2], 16)

            def move(n, slot):
                for b in range(2):
                    for part, source in enumerate((high, low)):
                        sp.dma_start(halves[slot][b][D * part:D * (part + 1), :], source[D * b:D * (b + 1), :])\
                          .then_inc(moved, 16)

            load(0, 0)
            sp.wait_ge(flat_ready, 3)
            move(0, 0)
            with sp.Fori(0, turns) as i:
                for k in range(2):
                    n = sp.snap(2 * i + k)
                    sp.wait_ge(closes, n * 3)
                    load(n + 1, (k + 1) % 2)
                    sp.wait_ge(flat_ready, n * 3 + 6)
                    move(n + 1, (k + 1) % 2)
                    for x in range(3):
                        emit(n, k, x)
            for k in range(2):
                sp.wait_ge(stored[k], 16 * EMITTED[k] * turns)
                sp.wait_ge(loaded[k], 32 * (turns + 1 - k))

        @block.gpsimd
        def _(pool):
            pool.memset(wparts[:, :], 0.0).then_inc(cleared, 1)

            pool.wait_ge(loaded[0], 32)
            pool.tensor_tensor(base[0][:, :], x2[0][:, :], h2[0][:, :], ALU.add).then_inc(based, 1)
            with pool.Fori(0, turns) as i:
                for k in range(2):
                    pool.wait_ge(closes, (2 * i + k) * 3)
                    pool.wait_ge(loaded[(k + 1) % 2], (i + 1 + k) * 32)
                    s = (k + 1) % 2
                    pool.tensor_tensor(base[s][:, :], x2[s][:, :], h2[s][:, :], ALU.add).then_inc(based, 1)

        @block.scalar
        def _(act):
            act.wait_ge(cleared, 1)

            def step(kind, x, n, k, slot, at, pair):
                if kind == "square":
                    act.wait_ge(loaded[slot], pair[1] * 32)
                    act.activation(squares[:, :], x2[slot][:, :], ACT.Square).then_inc(squared, 1)
                elif kind == "norm":
                    act.wait_ge(shared_read, at)
                    act.activation(rms[:, :], rms[:, :], ACT.Ln, bias=chip.v("rms_eps")).then_inc(rms_ready, 1)
                    act.wait_ge(rms_ready, pair[0] * 2 + 1)
                    act.activation(rms[:, :], rms[:, :], ACT.Exp, scale=-0.5).then_inc(rms_ready, 1)
                elif kind == "exponents":
                    act.wait_ge(shared_read, at)
                    act.activation(prob[:, :], logit[:, :], ACT.Exp).then_inc(exp_ready, 1)
                elif kind == "turn_weights":
                    act.wait_ge(shared_ready, at)
                    got = shared[:, :].bitcast(BF16)
                    if x == 0:
                        act.activation(turned[slot][0:96, 0:L], got[0:96, 0:L], ACT.Copy).then_inc(shared_read, 1)
                    else:
                        act.activation(turned[slot][0:96, L:TP], got[0:96, P - 2:P], ACT.Copy)\
                           .then_inc(shared_read, 1)

            source = {"norm": ("mean", 2), "exponents": ("route", 0)}
            for kind, x in E_PROLOGUE:
                if kind not in ("square", "norm", "exponents", "turn_weights"):
                    continue
                at = use_first(source.get(kind, (kind, x))) if kind != "square" else None
                step(kind, x, 0, 0, 0, at, (0, 1))
            with act.Fori(0, turns) as i:
                for k in range(2):
                    n = act.snap(2 * i + k)
                    for kind, x in E_ORDER:
                        if kind == "up":
                            r = x % HIDDEN_RING
                            rows_ = CHUNKS[x % 3][1]
                            act.wait_ge(up_a, n * UNITS + (x + 1))
                            act.wait_ge(hiddens, n * UNITS + max(x - HIDDEN_RING + 1, 0))
                            act.activation(gate[r][0:rows_, :], bank[A_BANKS[x % 2]][0:rows_, 0:THIRD], ACT.Silu,
                                           scale=chip.unscale[0:rows_, 0:1])\
                               .then_inc(gates, 1)
                        elif kind == "spread":
                            act.wait_ge(shared_ready, use(n, (kind, x)))
                            act.wait_ge(weighs, n * GROUPS + max(x - 1, 0))
                            act.activation(spread[x % 2][:, :], shared[:, 0:THIRD], ACT.Copy).then_inc(shared_read, 1)
                        elif kind in ("square", "norm", "exponents", "turn_weights"):
                            at = use(n, source.get(kind, (kind, x))) if kind != "square" else None
                            step(kind, x, n, k, (k + 1) % 2, at, (n + 1, i + 1 + k))

        @block.vector
        def _(dve):
            dve.wait_ge(cleared, 1)

            first_weight = groups(chip.const(C_FIRST, GR * NE))
            lg, pb, oh, sc, ot = (groups(x) for x in (logit, prob, one_hot, second, other))
            parts = wparts[:, :].rearrange("p (t a r) -> p t a r", t=9, a=3)
            w = prob[:, :].rearrange("p (t r) -> p t r", t=9)
            left = second[:, :].rearrange("p (t r) -> p t r", t=9)

            def choose(pair, x, at):
                before = pair * CHOSEN + max(2 * x - 1, 0)

                def then(ins, n=1):
                    ins.then_inc(chosen, 1)
                    if n == 1 and x > 0:
                        dve.wait_ge(chosen, before + 1)

                if x == 0:
                    raw = shared[:, 0:GR * NE].rearrange("p (g e) -> p g e", e=NE)
                    dve.wait_ge(shared_ready, at)
                    then(dve.tensor_reduce(best[:, :], raw, AX_X, ALU.max))
                    dve.wait_ge(chosen, before + 1)
                    dve.wait_ge(exp_ready, pair)
                    dve.tensor_tensor(lg, raw, to_all(best), ALU.subtract).then_inc(shared_read, 1)
                    return
                dve.wait_ge(chosen, before)
                if x == 1:
                    dve.wait_ge(exp_ready, pair + 1)
                    then(dve.tensor_reduce(per_group[:, :], pb, AX_X, ALU.add))
                    then(dve.reciprocal(per_group[:, :], per_group[:, :]), 2)
                elif x == 2:
                    then(dve.tensor_tensor(pb, pb, to_all(per_group), ALU.mult))
                    then(dve.tensor_reduce(best[:, :], pb, AX_X, ALU.max), 2)
                elif x == 3:
                    then(dve.tensor_tensor(oh, pb, to_all(best), ALU.is_equal))
                    then(dve.tensor_tensor(oh, oh, first_weight, ALU.mult), 2)
                elif x == 4:
                    then(dve.tensor_reduce(per_group[:, :], oh, AX_X, ALU.max))
                    then(dve.tensor_tensor(oh, oh, to_all(per_group), ALU.is_equal), 2)
                elif x == 5:
                    then(dve.scalar_tensor_tensor(second[:, :], one_hot[:, :], -2.0, prob[:, :], ALU.mult, ALU.add))
                    then(dve.tensor_reduce(best2[:, :], sc, AX_X, ALU.max), 2)
                elif x == 6:
                    then(dve.tensor_tensor(ot, sc, to_all(best2), ALU.is_equal))
                    then(dve.tensor_tensor(ot, ot, first_weight, ALU.mult), 2)
                elif x == 7:
                    then(dve.tensor_reduce(per_group[:, :], ot, AX_X, ALU.max))
                    then(dve.tensor_tensor(ot, ot, to_all(per_group), ALU.is_equal), 2)
                elif x == 8:
                    then(dve.tensor_tensor(oh, oh, ot, ALU.add))
                    then(dve.tensor_tensor(pb, pb, oh, ALU.mult), 2)
                elif x == 9:
                    then(dve.scalar_tensor_tensor(per_group[:, :], best[:, :], 1e-9, best2[:, :], ALU.add, ALU.add))
                    then(dve.reciprocal(per_group[:, :], per_group[:, :]), 2)
                elif x == 10:
                    then(dve.tensor_tensor(pb, pb, to_all(per_group), ALU.mult))
                    then(dve.tensor_copy(parts[:, :, 0, 0:16], w), 2)
                elif x == 11:
                    then(dve.tensor_tensor(left, w, parts[:, :, 0, 0:16], ALU.subtract))
                    then(dve.tensor_copy(parts[:, :, 1, 0:16], left), 2)
                else:
                    then(dve.tensor_tensor(left, left, parts[:, :, 1, 0:16], ALU.subtract))
                    then(dve.tensor_copy(parts[:, :, 2, 0:16], left), 2)

            def prepare(kind, x, pair, slot, at):
                if kind == "mean":
                    dve.wait_ge(shared_ready, at)
                    if x == 0:
                        dve.wait_ge(flat_ready, pair * 3)
                    dve.tensor_copy(third(rms, x), shared[:, 0:THIRD]).then_inc(shared_read, 1)
                elif kind == "norm":
                    dve.wait_ge(rms_ready, pair * 2 + 2)
                    dve.tensor_tensor(flat[:, :], x2[slot][:, :], rms[:, :], ALU.mult).then_inc(flat_ready, 1)
                elif x == 0:
                    dve.wait_ge(moved, pair * 64)
                    dve.scalar_tensor_tensor(high[:, :], x2[slot][:, :], X_SCALE, rms[:, :], ALU.mult, ALU.mult)\
                       .then_inc(flat_ready, 1)
                else:
                    dve.wait_ge(flat_ready, pair * 3 + 2)
                    dve.scalar_tensor_tensor(low[:, :], flat[:, :], X_SCALE, high[:, :], ALU.mult, ALU.subtract)\
                       .then_inc(flat_ready, 1)

            for kind, x in E_PROLOGUE:
                if kind in ("mean", "norm", "split"):
                    prepare(kind, x, 0, 0, use_first((kind, x)) if kind == "mean" else None)
            for x in range(CHOICES):
                choose(0, x, use_first(("route", 0)))
            with dve.Fori(0, turns) as i:
                for k in range(2):
                    n = dve.snap(2 * i + k)
                    for kind, x in E_ORDER:
                        if kind == "up":
                            r = x % HIDDEN_RING
                            rows_ = CHUNKS[x % 3][1]
                            dve.wait_ge(up_b, n * UNITS + (x + 1))
                            dve.wait_ge(gates, n * UNITS + (x + 1))
                            dve.wait_ge(downs, n * UNITS + max(x - HIDDEN_RING + 1, 0))
                            dve.scalar_tensor_tensor(hidden[r][0:rows_, :], bank[B_BANKS[x % 2]][0:rows_, 0:THIRD],
                                                     chip.unscale[0:rows_, 1:2], gate[r][0:rows_, :],
                                                     ALU.mult, ALU.mult).then_inc(hiddens, 1)
                        elif kind == "weigh":
                            dve.wait_ge(downs, n * UNITS + 3 * (x + 1))
                            dve.wait_ge(shared_read, use(n, ("spread", x)))
                            dve.wait_ge(folds, n * GROUPS + max(x - 1, 0))
                            dve.tensor_tensor(weighed[x % 2][:, :], bank[OUT_BANKS[x % 2]][:, 0:THIRD],
                                              spread[x % 2][:, :], ALU.mult).then_inc(weighs, 1)
                        elif kind == "close":
                            dve.wait_ge(folds, n * GROUPS + (x + 1) * G_THIRD)
                            dve.wait_ge(based, n + 1)
                            dve.tensor_tensor(third(whole, x), third(base[k], x), total[:, 0:THIRD], ALU.add)\
                               .then_inc(closes, 1)
                        elif kind == "emit":
                            r = (k + x) % 2
                            dve.wait_ge(shared_ready, use(n, (kind, x)))
                            dve.wait_ge(stored[r], emitted_before(i, k, x))
                            full = len([t for t in EMIT_TILES[x] if t < TILES]) * P
                            if x == 2:
                                dve.tensor_copy(outs[r][0:1, full:full + P], shared[0:1, full:full + P])
                            dve.tensor_copy(outs[r][:, 0:full], shared[:, 0:full]).then_inc(shared_read, 1)
                        elif kind in ("mean", "norm", "split"):
                            prepare(kind, x, n + 1, (k + 1) % 2, use(n, (kind, x)) if kind == "mean" else None)
                        elif kind == "choose":
                            choose(n + 1, x, use(n, ("route", 0)))

        @block.tensor
        def _(pe):
            pe.wait_ge(cleared, 1)

            def step(kind, x, slot, at, pair):
                if kind == "mean":
                    pe.wait_ge(squared, pair + 1)
                    pe.wait_ge(shared_read, at - 1)
                    pe.matmul(shared[:, 0:THIRD], chip.const(C_MEAN), third(squares, x), start=True, stop=True)\
                      .then_inc(shared_ready, 1)
                elif kind == "route":
                    pe.wait_ge(flat_ready, pair * 3 + 1)
                    pe.wait_ge(shared_read, at - 1)
                    for t in range(9):
                        first = min(t * P, TP - P)
                        ins = pe.matmul(shared[:, t * 16:(t + 1) * 16], flat[:, first:first + P],
                                        chip.router[:, :], start=True, stop=True)
                    ins.then_inc(shared_ready, 1)
                elif kind == "turn_weights":
                    pe.wait_ge(chosen, (pair + 1) * CHOSEN)
                    pe.wait_ge(shared_read, at - 1)
                    for t in range(TILES) if x == 0 else (TILES,):
                        col = t % TILES * P
                        ins = pe.transpose(shared[:, :].bitcast(BF16)[0:96, col:col + P],
                                           wparts[:, t * 96:(t + 1) * 96], chip.ident16[:, :])
                    ins.then_inc(shared_ready, 1)

            for kind, x in E_PROLOGUE:
                if kind in E_SHARED_KINDS:
                    step(kind, x, 0, use_first((kind, x)), 0)
            with pe.Fori(0, turns) as i:
                for k in range(2):
                    n = pe.snap(2 * i + k)
                    for kind, x in E_ORDER:
                        if kind == "up":
                            c, b, p, m = unit(x)
                            rows_ = CHUNKS[m][1]
                            w = (p * 3 + m) * P
                            if x == 0:
                                pe.wait_ge(moved, n * 64 + 64)
                            for read, bk, weights, got in ((gates, A_BANKS, chip.w1, up_a),
                                                           (hiddens, B_BANKS, chip.w3, up_b)):
                                pe.wait_ge(read, n * UNITS + max(x - 1, 0))
                                for part in range(2):
                                    at = part * (PAIRS * 3 * P) + w
                                    ins = pe.matmul(bank[bk[x % 2]][0:rows_, 0:THIRD], weights[:, at:at + rows_],
                                                    third(halves[k][b], c), start=part == 0, stop=part == 1)
                                ins.then_inc(got, 1)
                        elif kind == "down":
                            c, b, p, m = unit(x)
                            rows_ = CHUNKS[m][1]
                            g = x // 3
                            outputs = (slice(0, D), slice(D, P), slice(0, P))[m]
                            w = (p * 3 + m) * P
                            pe.wait_ge(hiddens, n * UNITS + (x + 1))
                            if m == 0:
                                pe.wait_ge(weighs, n * GROUPS + max(g - 1, 0))
                            pe.matmul(bank[OUT_BANKS[g % 2]][outputs, 0:THIRD],
                                      chip.w2[0:rows_, w + outputs.start:w + outputs.stop],
                                      hidden[x % HIDDEN_RING][0:rows_, :], start=m < 2, stop=m == 2)\
                              .then_inc(downs, 1)
                        elif kind == "spread":
                            c, b, p, _ = unit(3 * x)
                            at = use(n, (kind, x))
                            pe.wait_ge(shared_read, at - 1)
                            w = (b * PAIRS + p) * P
                            pe.matmul(shared[:, 0:THIRD], chip.spread16[0:96, w:w + P], third(turned[k], c)[0:96],
                                      start=True, stop=True).then_inc(shared_ready, 1)
                        elif kind == "fold":
                            c, b, p, _ = unit(3 * x)
                            pe.wait_ge(weighs, n * GROUPS + (x + 1))
                            if x % G_THIRD == 0:
                                pe.wait_ge(closes, n * 3 + c)
                            pe.matmul(total[D * b:D * (b + 1), 0:THIRD], chip.const(C_FOLD, D),
                                      weighed[x % 2][:, :], start=p == 0, stop=p == PAIRS - 1).then_inc(folds, 1)
                        elif kind == "emit":
                            at = use(n, (kind, x))
                            pe.wait_ge(closes, n * 3 + (x + 1))
                            pe.wait_ge(shared_read, at - 1)
                            for a, t in enumerate(EMIT_TILES[x]):
                                tokens = P if t < TILES else 2
                                ins = pe.transpose(shared[0:tokens, a * P:(a + 1) * P],
                                                   whole[:, t * P:t * P + tokens], chip.const(C_IDENT))
                            ins.then_inc(shared_ready, 1)
                        elif kind in E_SHARED_KINDS:
                            step(kind, x, (k + 1) % 2, use(n, (kind, x)), n + 1)


def build(nc, dram):
    images = dram["x"].shape[0]
    for name, n in (("h", 0), ("mixed", 0), ("h2", 2), ("z", 1), ("hn", AHEAD), ("x2", 2)):
        dram[name] = nc.dram_tensor("scratch_" + name, [images + n, D, TP], F32, kind="Internal").ap()
    with ExitStack() as ctx:
        chip = Chip(nc, ctx, images)
        load_weights(nc, chip, dram)
        mix(nc, chip, dram, images)
        normalize(nc, chip, dram, images)
        attend(nc, chip, dram, images)
        route_and_mix_experts(nc, chip, dram, images)


def kernel(**inputs):
    import numpy as np
    import concourse.bacc as bacc
    from concourse.bass_utils import run_bass_kernel_spmd

    nc = bacc.Bacc("TRN2", target_bir_lowering=False, num_devices=1)
    arrays = {name: np.ascontiguousarray(a) for name, a in inputs.items()}
    arrays["shape_consts"] = shape_constants()
    dram = {name: nc.dram_tensor(name, a.shape, mybir.dt.from_np(a.dtype), kind="ExternalInput").ap()
            for name, a in arrays.items()}
    images = arrays["x"].shape[0]
    dram["out"] = nc.dram_tensor("out", (images, T, D), F32, kind="ExternalOutput").ap()
    build(nc, dram)
    result = run_bass_kernel_spmd(nc, [arrays], core_ids=[0])
    return result.results[0]["out"]
```

```python
from contextlib import ExitStack

import concourse.bass as bass
from concourse import mybir

F32 = mybir.dt.float32
BF16 = mybir.dt.bfloat16
F16 = mybir.dt.float16
ALU = mybir.AluOpType
ACT = mybir.ActivationFunctionType
AX_X = mybir.AxisListType.X

P = 128
D = 64
IMG, PATCH = 224, 7
GRID = IMG // PATCH
PIX = PATCH * PATCH
L = GRID * GRID
T = L + 1
TP = T + 1
THIRD = TP // 3
STATE = 16
TAPS = 4
NH, NKV, HD = 4, 2, 16
QK = (NH + NKV) * HD
TILES = 8
NE, HID = 8, 170
PAIRS = NE // 2
CHUNKS = ((0, 114), (228, 112), (114, 114))
X_SCALE, W_TOP = 2.0 ** 12, 2.0 ** 14
START = 1
LN_EPS, RMS_EPS, BN_EPS = 1e-5, 1e-6, 1e-5
MASKED = -1e30
XCOLS = IMG - PATCH + 1

C_IDENT = 0
C_MEAN = C_IDENT + P
C_HALF = C_MEAN + P
C_FOLD = C_HALF + P
C_DEN = C_FOLD + P
C_MASK_Q = C_DEN + P
C_MASK_K = C_MASK_Q + P
C_SPREAD = C_MASK_K + P
C_FIRST = C_SPREAD + 2 * PAIRS * P
C_COS = C_FIRST + 9 * 2 * NE
C_SIN = C_COS + TP
C_END = C_SIN + TP

AHEAD = 3


def thirds(ap):
    return ap.rearrange("p (c n) -> p c n", c=3)


def shape_constants():
    import numpy as np

    c = np.zeros((P, C_END), np.float32)
    eye = np.eye(P, dtype=np.float32)
    half = np.arange(P) // D
    c[:, C_IDENT:C_IDENT + P] = eye
    c[:, C_MEAN:C_MEAN + P] = (half[:, None] == half[None, :]) / D
    c[:, C_HALF:C_HALF + P] = 0.5 * (np.arange(P)[:, None] % D == np.arange(P)[None, :] % D)
    same = (np.arange(P)[:, None] % D == np.arange(D)[None, :]).astype(np.float32)
    c[:, C_FOLD:C_FOLD + D] = same
    c[:, C_DEN:C_DEN + P] = np.arange(P)[:, None] == 32 * (np.arange(P)[None, :] // 32) + HD
    later = np.arange(P)[None, :] > np.arange(P)[:, None]
    c[:, C_MASK_Q:C_MASK_Q + P] = np.where(later, MASKED, 0)
    c[:, C_MASK_K:C_MASK_K + P] = np.where(later.T, MASKED, 0)
    for b in range(2):
        for p in range(PAIRS):
            for part in range(3):
                for m in range(P):
                    c[part * 32 + b * NE + 2 * p + m // D, C_SPREAD + (b * PAIRS + p) * P + m] = 1
    c[:, C_FIRST:C_COS] = np.tile(NE - np.arange(NE), 9 * 2)
    inv_freq = 1.0 / 10000.0 ** (np.arange(0, HD, 2, dtype=np.float32) / HD)
    freqs = np.outer(np.arange(TP, dtype=np.float32), inv_freq.astype(np.float32))
    cos, sin = np.cos(freqs).T, np.sin(freqs).T
    c[0:QK, C_COS:C_COS + TP] = np.tile(cos, (2 * (NH + NKV), 1))
    c[0:QK, C_SIN:C_SIN + TP] = np.tile(np.concatenate([-sin, sin]), (NH + NKV, 1))
    return c


def start_counts(nc, counts):
    with nc.Block() as block:
        @block.gpsimd
        def _(pool):
            for x in counts:
                pool.sem_inc(x, START)


class Chip:

    def __init__(self, nc, ctx, images):
        def sb(name, cols, dt=F32):
            return ctx.enter_context(nc.sbuf_tensor(name, [P, cols], dt))

        self.consts = sb("consts", C_END)
        self.vec = sb("vec", 32)
        self.pos = sb("pos", TP)
        self.tok_w = sb("tok_w", P)
        self.in_p = sb("in_p", P)
        self.in_r = sb("in_r", P)
        self.out_w = sb("out_w", P)
        self.dt_w = sb("dt_w", 2 * STATE)
        self.b_w = sb("b_w", 2 * STATE)
        self.c_w = sb("c_w", P)
        self.qk_w = sb("qk_w", QK)
        self.qk_swapped = sb("qk_swapped", QK)
        self.v_w = sb("v_w", NKV * HD)
        self.o_w = sb("o_w", D)
        self.router = sb("router", 2 * NE)
        self.w1 = sb("w1", 2 * PAIRS * 3 * P, F16)
        self.w3 = sb("w3", 2 * PAIRS * 3 * P, F16)
        self.unscale = sb("unscale", 2)
        self.w2 = sb("w2", PAIRS * 3 * P)
        self.ident16 = sb("ident16", P, BF16)
        self.mask_q16 = sb("mask_q16", P, BF16)
        self.mask_k16 = sb("mask_k16", P, BF16)
        self.spread16 = sb("spread16", 2 * PAIRS * P, BF16)
        self.stats = sb("stats", (images // 2) * 3 * 6)
        self.psum = ctx.enter_context(nc.psum_tensor("psum", [P, 8, 512], F32))
        self.bank = [self.psum[:, i, :] for i in range(8)]

    def thirds(self, first):
        return self.psum[:, first:first + 3, 0:THIRD]

    def const(self, at, n=P):
        return self.consts[:, at:at + n]

    def v(self, name):
        i = VEC.index(name)
        return self.vec[:, i:i + 1]


VEC = ["tok_b", "in_b_p", "in_b_r", "conv_b", "out_b", "gamma", "beta", "ln1", "ln2",
       "tap0", "tap1", "tap2", "tap3", "ln_eps", "rms_eps", "bn_a", "bn_b", "cls", "eps_product"]


def load_weights(nc, chip, dram):
    consts, vec = chip.consts, chip.vec
    with ExitStack() as ctx:
        def sem(name):
            return ctx.enter_context(nc.semaphore(name))

        def natural(name, cols):
            return ctx.enter_context(nc.sbuf_tensor("nat_" + name, [P, cols], F32))

        n_small = natural("small", 9 * P)
        tok, in_p, in_r, out_w, qk, qk_s, v_o, router, b_w = (
            n_small[:, i * P:(i + 1) * P] for i in range(9))
        n_o = natural("o", P)
        n_c = natural("c", 2 * STATE)
        n_pos = natural("pos", TILES * P)
        n_w1 = natural("w1", PAIRS * 3 * P)
        n_w3 = natural("w3", PAIRS * 3 * P)
        n_w2 = natural("w2", PAIRS * 2 * HID)
        w1, w3 = natural("w1_turned", PAIRS * 3 * P), natural("w3_turned", PAIRS * 3 * P)
        ones, largest, smallest, scale, peak, diag = (natural(x, n) for x, n in (
            ("ones", P), ("largest", 2), ("smallest", 2), ("scale", 2), ("peak", 1), ("diag", 2)))

        cleared = [n_small[:, :], n_o[:, :], n_c[:, :], n_w2[:, :], chip.dt_w[:, :], w1[:, :], w3[:, :],
                   chip.w2[:, :], chip.pos[:, :], chip.v("ln_eps"), chip.v("rms_eps"), ones[:, :],
                   chip.v("eps_product")]
        values = {9: LN_EPS, 10: RMS_EPS, 11: 1.0, 12: RMS_EPS * LN_EPS}

        turns = [
            (tok, chip.tok_w[:, :], None),
            (in_p, chip.in_p[:, :], None),
            (in_r, chip.in_r[:, :], None),
            (out_w, chip.out_w[:, :], None),
            (qk[0:QK, :], chip.qk_w[:, :], "ln1"),
            (qk_s[0:QK, :], chip.qk_swapped[:, :], "ln1"),
            (v_o[0:NKV * HD, :], chip.v_w[:, :], "ln1"),
            (n_o[0:D, :], chip.o_w[:, :], None),
            (router[0:2 * NE, :], chip.router[:, :], "ln2"),
            (b_w[0:2 * STATE, :], chip.b_w[:, :], None),
            (n_c[:, :], chip.c_w[0:2 * STATE, :], None),
        ]
        turns += [(n_pos[:, j * P:(j + 1) * P], chip.pos[:, 1 + j * P:1 + (j + 1) * P], "tok_b")
                  for j in range(TILES)]
        for i in range(PAIRS * 3):
            first, rows = CHUNKS[i % 3]
            for n, w in ((n_w1, w1), (n_w3, w3)):
                turns.append((n[0:rows, i * P:(i + 1) * P], w[:, i * P:i * P + rows], "ln2"))
            at = i // 3 * 2 * HID + first
            turns.append((n_w2[:, at:at + rows], chip.w2[0:rows, i * P:(i + 1) * P], None))

        cleared_all = sem("cleared_all")
        loaded = sem("loaded")
        turned = sem("turned")
        copied = sem("copied")
        scaled = sem("scaled")
        peaks = sem("peaks")
        bank = chip.bank

        def w_dram(name, m):
            w = dram[name]
            return bass.AP(w.tensor, CHUNKS[m][0] * D, [[D, CHUNKS[m][1]], [2 * HID * D, PAIRS], [1, D]])

        def column(name, n=D, step=1, offset=0):
            return bass.AP(dram[name].tensor, offset, [[step, n], [1, 1]])

        loads = [(consts[:, :], dram["shape_consts"])]
        for b in range(2):
            r = slice(D * b, D * (b + 1))
            e = slice(NE * b, NE * (b + 1))
            s = slice(STATE * b, STATE * (b + 1))
            loads += [
                (tok[r, D * b:D * b + PIX], dram["L0_tok_W"]),
                (in_p[r, r], dram["L0_attn_in_w"][0:D, :]),
                (in_r[r, r], dram["L0_attn_in_w"][D:2 * D, :]),
                (out_w[r, r], dram["L0_attn_out_w"]),
                (router[e, r], dram["L0_ffn_router_w"]),
                (b_w[s, r], dram["L0_attn_B_w"]),
                (n_c[r, s], dram["L0_attn_C_w"]),
                (chip.dt_w[r, s], dram["L0_attn_dt"]),
                (n_pos[:, :].rearrange("p (j u d) -> p j u d", j=TILES, u=2)[:, :, b, :],
                 dram["L0_tok_pos"][0].rearrange("(j p) d -> p j d", p=P)),
                (vec[r, 9:13], dram["L0_attn_conv_w"].rearrange("d a k -> d (a k)")),
            ]
            loads += [(vec[r, VEC.index(v):VEC.index(v) + 1], column(*src)) for v, src in {
                "tok_b": ("L0_tok_b",), "in_b_p": ("L0_attn_in_b",), "in_b_r": ("L0_attn_in_b", D, 1, D),
                "conv_b": ("L0_attn_conv_b",), "out_b": ("L0_attn_out_b",), "gamma": ("L0_attn_gamma",),
                "beta": ("L0_attn_beta",), "ln1": ("L0_ffn_ln1_w",), "ln2": ("L0_ffn_ln2_w",),
                "cls": ("cls_tok",)}.items()]
            for n, name in ((n_w1, "L0_ffn_w1"), (n_w3, "L0_ffn_w3")):
                to = n[:, :].rearrange("p (q m u d) -> p q m u d", q=PAIRS, m=3, u=2)
                loads += [(to[0:CHUNKS[m][1], :, m, b, :], w_dram(name, m)) for m in range(3)]
            loads.append((n_w2[r, :].rearrange("c (q u h) -> c q u h", q=PAIRS, u=2)[:, :, b, :],
                          bass.AP(dram["L0_ffn_w2"].tensor, b * D * HID,
                                  [[HID, D], [2 * D * HID, PAIRS], [1, HID]])))
        loads += [(qk[0:NH * HD, 0:D], dram["L0_ffn_wq"]), (qk[NH * HD:QK, 0:D], dram["L0_ffn_wk"]),
                  (v_o[0:NKV * HD, 0:D], dram["L0_ffn_wv"])]
        for h in range(NH + NKV):
            w, g = (dram["L0_ffn_wq"], h) if h < NH else (dram["L0_ffn_wk"], h - NH)
            half = HD // 2
            loads += [(qk_s[HD * h:HD * h + half, 0:D], w[HD * g + half:HD * (g + 1), :]),
                      (qk_s[HD * h + half:HD * (h + 1), 0:D], w[HD * g:HD * g + half, :])]
        loads.append((n_o[0:D, :].rearrange("o (h r) -> o h r", h=NH)[:, :, 0:HD],
                      dram["L0_ffn_wo"].rearrange("o (h r) -> o h r", h=NH)))

        block = ctx.enter_context(nc.Block())

        @block.gpsimd
        def _(pool):
            for i, ap in enumerate(cleared):
                pool.memset(ap, values.get(i, 0.0)).then_inc(cleared_all, 1)

        @block.sync
        def _(sp):
            sp.wait_ge(cleared_all, len(cleared))
            for to, src in loads[0::2]:
                sp.dma_start(to, src).then_inc(loaded, 16)

        @block.scalar
        def _(act):
            act.wait_ge(cleared_all, len(cleared))
            for to, src in loads[1::2]:
                act.dma_start(to, src).then_inc(loaded, 16)

        @block.tensor
        def _(pe):
            pe.wait_ge(cleared_all, len(cleared))
            pe.wait_ge(loaded, 16 * len(loads))
            for i, (src, _, _) in enumerate(turns):
                rows, cols = src.shape
                if i >= 8:
                    pe.wait_ge(copied, i - 7)
                pe.transpose(bank[i % 8][0:cols, 0:rows], src, chip.const(C_IDENT)[0:rows, 0:rows])\
                    .then_inc(turned, 1)
            pe.wait_ge(scaled, 5)
            pe.wait_ge(copied, len(turns))
            pe.transpose(bank[0][0:2, 0:P], largest[:, :], chip.const(C_IDENT)).then_inc(peaks, 1)
            pe.wait_ge(scaled, 7)
            pe.matmul(bank[1][:, 0:2], ones[0:2, :], diag[0:2, :], start=True, stop=True).then_inc(peaks, 1)

        @block.vector
        def _(dve):
            dve.wait_ge(cleared_all, len(cleared))
            dve.wait_ge(loaded, 16 * len(loads))
            for i, (src, to, by) in enumerate(turns):
                rows, cols = src.shape
                got = bank[i % 8][0:cols, 0:rows]
                dve.wait_ge(turned, i + 1)
                if by is None:
                    ins = dve.tensor_copy(to, got)
                else:
                    ins = dve.tensor_scalar(to, got, chip.v(by), None, ALU.add if by == "tok_b" else ALU.mult)
                ins.then_inc(copied, 1)
            n = len(turns)
            dve.tensor_copy(chip.pos[:, 0:1], chip.v("cls")).then_inc(copied, 1)
            for to, at in ((chip.ident16, C_IDENT), (chip.mask_q16, C_MASK_Q), (chip.mask_k16, C_MASK_K)):
                dve.tensor_copy(to[:, :], chip.const(at)).then_inc(copied, 1)
            dve.tensor_copy(chip.spread16[:, :], chip.const(C_SPREAD, 2 * PAIRS * P)).then_inc(copied, 1)
            dve.wait_ge(copied, n + 5)

            for k, w in enumerate((w1, w3)):
                dve.tensor_reduce(largest[:, k:k + 1], w[:, :], AX_X, ALU.max).then_inc(scaled, 1)
                dve.tensor_reduce(smallest[:, k:k + 1], w[:, :], AX_X, ALU.min).then_inc(scaled, 1)
            dve.wait_ge(scaled, 4)
            dve.scalar_tensor_tensor(largest[:, :], smallest[:, :], -1.0, largest[:, :], ALU.mult, ALU.max)\
               .then_inc(scaled, 1)
            dve.wait_ge(peaks, 1)
            dve.tensor_reduce(peak[0:2, :], bank[0][0:2, 0:P], AX_X, ALU.max).then_inc(scaled, 1)
            dve.wait_ge(scaled, 6)
            dve.tensor_scalar(diag[0:2, :], chip.const(C_IDENT)[0:2, 0:2], peak[0:2, :], None, ALU.mult)\
               .then_inc(scaled, 1)
            dve.wait_ge(peaks, 2)
            dve.tensor_scalar(largest[:, :], bank[1][:, 0:2], 1e-30, None, ALU.max).then_inc(scaled, 1)
            dve.wait_ge(scaled, 8)
            dve.reciprocal(scale[:, :], largest[:, :]).then_inc(scaled, 1)
            dve.tensor_scalar(chip.unscale[:, :], largest[:, :], 1.0 / (W_TOP * X_SCALE), None, ALU.mult)\
               .then_inc(scaled, 1)
            dve.wait_ge(scaled, 9)
            dve.tensor_scalar(scale[:, :], scale[:, :], W_TOP, None, ALU.mult).then_inc(scaled, 1)
            dve.wait_ge(scaled, 11)
            for k, (w, to) in enumerate(((w1, chip.w1), (w3, chip.w3))):
                half = PAIRS * 3 * P
                by = scale[:, k:k + 1]
                dve.tensor_scalar(to[:, 0:half], w[:, :], by, None, ALU.mult).then_inc(scaled, 1)
                dve.wait_ge(scaled, 12 + 2 * k)
                dve.scalar_tensor_tensor(to[:, half:], w[:, :], by, to[:, 0:half], ALU.mult, ALU.subtract)\
                   .then_inc(scaled, 1)
            dve.wait_ge(scaled, 15)


def mix(nc, chip, dram, images):
    turns = images // 4
    h_dram, o_dram = dram["h"], dram["mixed"]
    bank = chip.bank
    with ExitStack() as ctx:
        counts = []

        def sem(name):
            counts.append(ctx.enter_context(nc.semaphore(name)))
            return counts[-1]

        def two(name, cols):
            return [ctx.enter_context(nc.sbuf_tensor(f"{name}{k}", [P, cols], F32)) for k in range(2)]

        pixels, h, xc, sq, rstd, u = two("pixels", GRID * XCOLS), two("h", TP), two("xc", TP), two("sq", TP), \
            two("rstd", TP), two("u", TP)
        gate, xp, xconv, o = two("gate", TP), two("xp", TP + TAPS - 1), two("xconv", TP), two("o", TP)
        decay, scan = two("decay", TP), two("scan", TP)
        g, states, y = sq, rstd, xc
        ones = ctx.enter_context(nc.sbuf_tensor("ones", [P, TP], F32))
        S = 2 * STATE

        pixels_cleared = sem("pixels_cleared")
        preset = sem("preset")
        pixels_loaded = [sem("pixels_loaded0"), sem("pixels_loaded1")]
        h_stored = [sem("h_stored0"), sem("h_stored1")]
        o_stored = [sem("o_stored0"), sem("o_stored1")]
        names = """embedded h_ready mean_ready xc_ready sq_ready var_ready log_ready rstd_ready u_ready
            res_ready gate_ready xp_summed xp_ready conv_steps xconv_ready dt_ready decay_ready b_ready
            scan_ready bx_ready first_ready states_ready carried_ready y_ready c_ready g_ready out_ready
            o_ready stats_ready""".split()
        s = {name: sem(name) for name in names}

        def load(sp, i, k):
            for b in range(2):
                for p in range(PATCH):
                    first = (4 * i + 2 * k + b) * (IMG * IMG) + p * IMG
                    src = bass.AP(dram["x"].tensor, first, [[1, PATCH], [PATCH * IMG, GRID], [1, XCOLS]])
                    to = pixels[k][D * b + PATCH * p:D * b + PATCH * (p + 1), :]
                    sp.dma_start(to.rearrange("r (n c) -> r n c", n=GRID), src).then_inc(pixels_loaded[k], 16)

        start_counts(nc, counts)
        block = ctx.enter_context(nc.Block())

        @block.sync
        def _(sp):
            def store(i):
                for ready, stored, tile, to in (("h_ready", h_stored, h, h_dram), ("o_ready", o_stored, o, o_dram)):
                    for k in range(2):
                        sp.wait_ge(s[ready], START + 2 * i + k + 1)
                        sp.dma_start(bass.AP(to.tensor, (4 * i + 2 * k) * (D * TP), [[TP, P], [1, TP]]),
                                     tile[k][:, :]).then_inc(stored[k], 16)

            for k in range(2):
                sp.wait_ge(pixels_cleared, START + 2)
                load(sp, 0, k)
            if turns > 1:
                with sp.Fori(0, turns - 1) as i:
                    for k in range(2):
                        sp.wait_ge(s["embedded"], START + 2 * i + k + 1)
                        load(sp, i + 1, k)
                    store(i)
            store(turns - 1)
            for k in range(2):
                sp.wait_ge(h_stored[k], START + 16 * turns)
                sp.wait_ge(o_stored[k], START + 16 * turns)

        @block.gpsimd
        def _(pool):
            pool.memset(pixels[0][:, :], 0.0).then_inc(pixels_cleared, 1)
            pool.memset(ones[:, :], 1.0).then_inc(preset, 1)
            for k in range(2):
                pool.memset(xp[k][:, 0:TAPS - 1], 0.0).then_inc(preset, 1)

        @block.scalar
        def _(act):
            act.wait_ge(preset, START + 3)
            with act.Fori(0, turns) as i:
                n = [act.snap(2 * i + k + 1) for k in range(2)]
                for k in range(2):
                    act.wait_ge(s["xc_ready"], START + n[k])
                    act.activation(sq[k][:, :], xc[k][:, :], ACT.Square).then_inc(s["sq_ready"], 1)
                for k in range(2):
                    act.wait_ge(s["var_ready"], START + n[k])
                    act.activation(thirds(rstd[k][:, :]), chip.thirds(3 * k), ACT.Ln,
                                   bias=chip.v("ln_eps")).then_inc(s["log_ready"], 1)
                for k in range(2):
                    act.wait_ge(s["log_ready"], START + n[k])
                    act.activation(rstd[k][:, :], rstd[k][:, :], ACT.Exp, scale=-0.5).then_inc(s["rstd_ready"], 1)
                for k in range(2):
                    act.wait_ge(s["res_ready"], START + n[k])
                    act.activation(thirds(gate[k][:, :]), chip.thirds(3 * k), ACT.Silu,
                                   bias=chip.v("in_b_r")).then_inc(s["gate_ready"], 1)
                for k in range(2):
                    act.wait_ge(s["xp_summed"], START + n[k])
                    act.activation(thirds(xp[k][:, TAPS - 1:]), chip.thirds(3 * k), ACT.Identity,
                                   bias=chip.v("in_b_p")).then_inc(s["xp_ready"], 1)
                for k in range(2):
                    act.wait_ge(s["dt_ready"], START + n[k])
                    act.activation(thirds(decay[k][0:S, :]), chip.thirds(3 * k)[0:S], ACT.Exp)\
                       .then_inc(s["decay_ready"], 1)

        @block.vector
        def _(dve):
            dve.memset(pixels[1][:, :], 0.0).then_inc(pixels_cleared, 1)
            dve.wait_ge(preset, START + 3)
            for k in range(2):
                dve.tensor_copy(h[k][:, 0:1], chip.pos[:, 0:1]).then_inc(preset, 1)
                dve.tensor_copy(h[k][:, T:TP], chip.pos[:, T:TP]).then_inc(preset, 1)
            dve.wait_ge(preset, START + 7)
            with dve.Fori(0, turns) as i:
                n = [dve.snap(2 * i + k + 1) for k in range(2)]
                for k in range(2):
                    dve.wait_ge(s["embedded"], START + n[k])
                    dve.wait_ge(h_stored[k], START + 16 * i)
                    dve.tensor_tensor(h[k][:, 1:T].rearrange("p (c n) -> p c n", c=2),
                                      chip.psum[:, 3 * k:3 * k + 2, :],
                                      chip.pos[:, 1:T].rearrange("p (c n) -> p c n", c=2), ALU.add)\
                       .then_inc(s["h_ready"], 1)
                for k in range(2):
                    dve.wait_ge(s["mean_ready"], START + n[k])
                    dve.tensor_tensor(thirds(xc[k][:, :]), thirds(h[k][:, :]), chip.thirds(3 * k), ALU.subtract)\
                       .then_inc(s["xc_ready"], 1)
                for k in range(2):
                    dve.wait_ge(s["rstd_ready"], START + n[k])
                    dve.tensor_tensor(u[k][:, :], xc[k][:, :], rstd[k][:, :], ALU.mult).then_inc(s["u_ready"], 1)
                for k in range(2):
                    dve.wait_ge(s["xp_ready"], START + n[k])
                    dve.tensor_scalar(xconv[k][:, :], xp[k][:, 0:TP], chip.v("tap0"), chip.v("conv_b"),
                                      ALU.mult, ALU.add).then_inc(s["conv_steps"], 1)
                    for t in range(1, TAPS):
                        dve.wait_ge(s["conv_steps"], START + (2 * i + k) * (TAPS - 1) + t)
                        dve.scalar_tensor_tensor(xconv[k][:, :], xp[k][:, t:t + TP], chip.v(f"tap{t}"),
                                                 xconv[k][:, :], ALU.mult, ALU.add)\
                           .then_inc(s["conv_steps" if t < TAPS - 1 else "xconv_ready"], 1)
                for k in range(2):
                    dve.wait_ge(s["decay_ready"], START + n[k])
                    dve.tensor_tensor_scan(scan[k][0:S, :], decay[k][0:S, :], ones[0:S, :], 1.0, ALU.mult, ALU.mult)\
                       .then_inc(s["scan_ready"], 1)
                for k in range(2):
                    dve.wait_ge(s["b_ready"], START + n[k])
                    dve.wait_ge(s["scan_ready"], START + n[k])
                    dve.tensor_tensor(thirds(scan[k][0:S, :]), thirds(scan[k][0:S, :]),
                                      chip.thirds(3 * k)[0:S], ALU.mult).then_inc(s["bx_ready"], 1)
                    dve.tensor_copy(y[k][0:S, 0:1], chip.bank[3 * k][0:S, 0:1]).then_inc(s["first_ready"], 1)
                for k in range(2):
                    dve.wait_ge(s["bx_ready"], START + n[k])
                    dve.tensor_tensor_scan(states[k][0:S, :], ones[0:S, :], scan[k][0:S, :], 0.0, ALU.mult, ALU.add)\
                       .then_inc(s["states_ready"], 1)
                for k in range(2):
                    dve.wait_ge(s["states_ready"], START + n[k])
                    dve.tensor_tensor(scan[k][0:S, 1:TP], states[k][0:S, 0:TP - 1], decay[k][0:S, 1:TP], ALU.mult)\
                       .then_inc(s["carried_ready"], 1)
                for k in range(2):
                    dve.wait_ge(s["carried_ready"], START + n[k])
                    dve.wait_ge(s["first_ready"], START + n[k])
                    dve.tensor_tensor(y[k][0:S, 1:TP], states[k][0:S, 1:TP], scan[k][0:S, 1:TP], ALU.subtract)\
                       .then_inc(s["y_ready"], 1)
                for k in range(2):
                    dve.wait_ge(s["c_ready"], START + n[k])
                    dve.wait_ge(s["gate_ready"], START + n[k])
                    dve.tensor_tensor(thirds(g[k][:, :]), chip.thirds(3 * k), thirds(gate[k][:, :]), ALU.mult)\
                       .then_inc(s["g_ready"], 1)
                for k in range(2):
                    dve.wait_ge(s["out_ready"], START + n[k])
                    dve.wait_ge(s["xconv_ready"], START + n[k])
                    dve.wait_ge(o_stored[k], START + 16 * i)
                    dve.scalar_tensor_tensor(thirds(o[k][:, :]), chip.thirds(3 * k), chip.v("out_b"),
                                             thirds(xconv[k][:, :]), ALU.add, ALU.add).then_inc(s["o_ready"], 1)
                for k in range(2):
                    dve.wait_ge(s["o_ready"], START + n[k])
                    for c in range(3):
                        part = o[k][:, c * THIRD:min((c + 1) * THIRD, T)]
                        at = (2 * i + k) * 18 + 6 * c
                        ins = dve.bn_stats(chip.stats[:, bass.ds(at, 6)], part)
                    ins.then_inc(s["stats_ready"], 1)

        @block.tensor
        def _(pe):
            pe.wait_ge(preset, START + 3)

            def product(k, w, x, rows=P, contracted=P, shift=0, start=True, stop=True):
                for c in range(3):
                    ins = pe.matmul(chip.bank[3 * k + c][0:rows, 0:THIRD], w[0:contracted],
                                    x[0:contracted, c * THIRD + shift:(c + 1) * THIRD + shift],
                                    start=start, stop=stop)
                return ins

            with pe.Fori(0, turns) as i:
                n = [pe.snap(2 * i + k + 1) for k in range(2)]
                for k in range(2):
                    pe.wait_ge(pixels_loaded[k], START + (i + 1) * (2 * PATCH * 16))
                    pe.wait_ge(s["o_ready"], START + 2 * i)
                    for c in range(2):
                        view = pixels[k][:, :].rearrange("r (n c) -> r n c", n=GRID)
                        ins = pe.matmul(chip.bank[3 * k + c], chip.tok_w[:, :],
                                        view[:, c * GRID // 2:(c + 1) * GRID // 2, 0:XCOLS:PATCH],
                                        start=True, stop=True)
                    ins.then_inc(s["embedded"], 1)
                for k in range(2):
                    pe.wait_ge(s["h_ready"], START + n[k])
                    product(k, chip.const(C_MEAN), h[k]).then_inc(s["mean_ready"], 1)
                for k in range(2):
                    pe.wait_ge(s["sq_ready"], START + n[k])
                    product(k, chip.const(C_MEAN), sq[k]).then_inc(s["var_ready"], 1)
                for k in range(2):
                    pe.wait_ge(s["u_ready"], START + n[k])
                    product(k, chip.in_r[:, :], u[k]).then_inc(s["res_ready"], 1)
                for k in range(2):
                    pe.wait_ge(s["gate_ready"], START + n[k])
                    product(k, chip.in_p[:, :], u[k]).then_inc(s["xp_summed"], 1)
                for k in range(2):
                    pe.wait_ge(s["xconv_ready"], START + n[k])
                    product(k, chip.dt_w[:, :], xconv[k], rows=S).then_inc(s["dt_ready"], 1)
                for k in range(2):
                    pe.wait_ge(s["decay_ready"], START + n[k])
                    product(k, chip.b_w[:, :], xconv[k], rows=S).then_inc(s["b_ready"], 1)
                for k in range(2):
                    pe.wait_ge(s["y_ready"], START + n[k])
                    product(k, chip.c_w[:, :], y[k], contracted=S).then_inc(s["c_ready"], 1)
                for k in range(2):
                    pe.wait_ge(s["g_ready"], START + n[k])
                    product(k, chip.out_w[:, :], g[k]).then_inc(s["out_ready"], 1)

def normalize(nc, chip, dram, images):
    turns = images // 4
    with ExitStack() as ctx:
        counts = []

        def sem(name):
            counts.append(ctx.enter_context(nc.semaphore(name)))
            return counts[-1]

        def two(name):
            return [ctx.enter_context(nc.sbuf_tensor(f"{name}{k}", [P, TP], F32)) for k in range(2)]

        def small(name, cols):
            return ctx.enter_context(nc.sbuf_tensor(name, [P, cols], F32))

        mixed, h_in, h, xc, sq, rstd, both_norms, z, hn = (
            two("n_" + x) for x in ("mixed", "h_in", "h", "xc", "sq", "rstd", "both_norms", "z", "hn"))
        own, both, spread, var = small("own", 2), small("both", 1), small("spread", 1), small("var", 1)

        loaded = [sem("n_loaded0"), sem("n_loaded1")]
        stored = [sem("n_stored0"), sem("n_stored1")]
        tail_stored = sem("tail_stored")
        batch = sem("batch")
        batch_summed = sem("batch_summed")
        batch_power = sem("batch_power")
        names = """scaled_ready h_ready mean_ready xc_ready sq_ready var_ready log_ready rstd_ready
            log2_ready norms_ready z_ready hn_ready""".split()
        s = {name: sem("n_" + name) for name in names}
        bank = chip.bank

        start_counts(nc, counts)
        block = ctx.enter_context(nc.Block())

        def rows(name, image):
            return bass.AP(dram[name].tensor, image * (D * TP), [[TP, P], [1, TP]])

        @block.sync
        def _(sp):
            def load(i, k):
                sp.dma_start(h_in[k][:, :], rows("h", 4 * i + 2 * k)).then_inc(loaded[k], 16)
                sp.dma_start(mixed[k][:, :], rows("mixed", 4 * i + 2 * k)).then_inc(loaded[k], 16)

            def store(i):
                for ready, tile, to in (("h_ready", h, "h2"), ("z_ready", z, "z"), ("hn_ready", hn, "hn")):
                    for k in range(2):
                        sp.wait_ge(s[ready], START + 2 * i + k + 1)
                        sp.dma_start(rows(to, 4 * i + 2 * k), tile[k][:, :]).then_inc(stored[k], 16)

            for k in range(2):
                load(0, k)
            if turns > 1:
                with sp.Fori(0, turns - 1) as i:
                    for k in range(2):
                        sp.wait_ge(s["h_ready"], START + 2 * i + k + 1)
                        load(i + 1, k)
                    store(i)
            store(turns - 1)
            for n in range(AHEAD):
                sp.dma_start(bass.AP(dram["hn"].tensor, (images + n) * D * TP, [[TP, D], [1, TP]]),
                             hn[0][0:D, :]).then_inc(tail_stored, 16)
            sp.dma_start(bass.AP(dram["z"].tensor, images * D * TP, [[TP, D], [1, TP]]),
                         hn[0][0:D, :]).then_inc(tail_stored, 16)
            for name in ("h2", "x2"):
                sp.dma_start(rows(name, images), hn[0][:, :]).then_inc(tail_stored, 16)
            sp.wait_ge(tail_stored, START + 16 * (AHEAD + 3))
            for k in range(2):
                sp.wait_ge(stored[k], START + 48 * turns)

        @block.tensor
        def _(pe):
            pe.wait_ge(batch, START + 1)
            pe.matmul(bank[6][:, 0:2], chip.const(C_HALF), own[:, :], start=True, stop=True).then_inc(batch_summed, 1)
            pe.wait_ge(batch, START + 4)
            pe.matmul(bank[6][:, 0:1], chip.const(C_HALF), spread[:, :], start=True, stop=True)\
              .then_inc(batch_summed, 1)

            def average(k, x):
                for c in range(3):
                    ins = pe.matmul(bank[3 * k + c][:, 0:THIRD], chip.const(C_MEAN),
                                    x[:, c * THIRD:(c + 1) * THIRD], start=True, stop=True)
                return ins

            with pe.Fori(0, turns) as i:
                n = [pe.snap(2 * i + k + 1) for k in range(2)]
                for k in range(2):
                    pe.wait_ge(s["h_ready"], START + n[k])
                    pe.wait_ge(s["log2_ready"], START + 2 * i)
                    average(k, h[k]).then_inc(s["mean_ready"], 1)
                for k in range(2):
                    pe.wait_ge(s["sq_ready"], START + n[k])
                    average(k, sq[k]).then_inc(s["var_ready"], 1)

        @block.scalar
        def _(act):
            act.wait_ge(batch, START + 5)
            act.activation(var[:, :], var[:, :], ACT.Ln).then_inc(batch_power, 1)
            act.wait_ge(batch_power, START + 1)
            act.activation(var[:, :], var[:, :], ACT.Exp, scale=-0.5).then_inc(batch_power, 1)
            act.wait_ge(batch, START + 8)
            with act.Fori(0, turns) as i:
                n = [act.snap(2 * i + k + 1) for k in range(2)]
                for k in range(2):
                    act.wait_ge(loaded[k], START + (i + 1) * 32)
                    act.wait_ge(s["h_ready"], START + 2 * i)
                    act.activation(mixed[k][:, :], mixed[k][:, :], ACT.Identity, scale=chip.v("bn_a"),
                                   bias=chip.v("bn_b")).then_inc(s["scaled_ready"], 1)
                for k in range(2):
                    act.wait_ge(s["xc_ready"], START + n[k])
                    act.activation(sq[k][:, :], xc[k][:, :], ACT.Square).then_inc(s["sq_ready"], 1)
                for k in range(2):
                    act.wait_ge(s["var_ready"], START + n[k])
                    act.activation(thirds(rstd[k][:, :]), chip.thirds(3 * k), ACT.Ln,
                                   bias=chip.v("ln_eps")).then_inc(s["log_ready"], 1)
                for k in range(2):
                    act.activation(thirds(both_norms[k][:, :]), chip.thirds(3 * k), ACT.Ln, scale=1.0 + RMS_EPS,
                                   bias=chip.v("eps_product")).then_inc(s["log2_ready"], 1)
                for k in range(2):
                    act.wait_ge(s["log_ready"], START + n[k])
                    act.activation(rstd[k][:, :], rstd[k][:, :], ACT.Exp, scale=-0.5).then_inc(s["rstd_ready"], 1)
                for k in range(2):
                    act.wait_ge(s["log2_ready"], START + n[k])
                    act.activation(both_norms[k][:, :], both_norms[k][:, :], ACT.Exp, scale=-0.5)\
                       .then_inc(s["norms_ready"], 1)

        @block.vector
        def _(dve):
            dve.bn_aggr(own[:, :], chip.stats[:, :].rearrange("p (n s) -> p n s", s=6)).then_inc(batch, 1)
            dve.wait_ge(batch_summed, START + 1)
            dve.tensor_copy(both[:, :], bank[6][:, 0:1]).then_inc(batch, 1)
            dve.wait_ge(batch, START + 2)
            dve.tensor_tensor(spread[:, :], own[:, 0:1], both[:, :], ALU.subtract).then_inc(batch, 1)
            dve.wait_ge(batch, START + 3)
            dve.scalar_tensor_tensor(spread[:, :], spread[:, :], spread[:, 0:1], own[:, 1:2], ALU.mult, ALU.add)\
               .then_inc(batch, 1)
            dve.wait_ge(batch_summed, START + 2)
            dve.tensor_scalar(var[:, :], bank[6][:, 0:1], BN_EPS, None, ALU.add).then_inc(batch, 1)
            dve.wait_ge(batch_power, START + 2)
            dve.tensor_tensor(chip.v("bn_a"), var[:, :], chip.v("gamma"), ALU.mult).then_inc(batch, 1)
            dve.wait_ge(batch, START + 6)
            dve.tensor_tensor(both[:, :], both[:, :], chip.v("bn_a"), ALU.mult).then_inc(batch, 1)
            dve.wait_ge(batch, START + 7)
            dve.tensor_tensor(chip.v("bn_b"), chip.v("beta"), both[:, :], ALU.subtract).then_inc(batch, 1)
            with dve.Fori(0, turns) as i:
                n = [dve.snap(2 * i + k + 1) for k in range(2)]
                for k in range(2):
                    dve.wait_ge(s["scaled_ready"], START + n[k])
                    dve.wait_ge(stored[k], START + 48 * i)
                    dve.tensor_tensor(h[k][:, :], h_in[k][:, :], mixed[k][:, :], ALU.add).then_inc(s["h_ready"], 1)
                for k in range(2):
                    dve.wait_ge(s["mean_ready"], START + n[k])
                    dve.tensor_tensor(thirds(xc[k][:, :]), thirds(h[k][:, :]), chip.thirds(3 * k), ALU.subtract)\
                       .then_inc(s["xc_ready"], 1)
                for k in range(2):
                    dve.wait_ge(s["rstd_ready"], START + n[k])
                    dve.tensor_tensor(z[k][:, :], xc[k][:, :], rstd[k][:, :], ALU.mult).then_inc(s["z_ready"], 1)
                for k in range(2):
                    dve.wait_ge(s["norms_ready"], START + n[k])
                    dve.tensor_tensor(hn[k][:, :], xc[k][:, :], both_norms[k][:, :], ALU.mult)\
                       .then_inc(s["hn_ready"], 1)



HI, MID, LO = range(3)
Q_TERMS = (HI, HI, MID, HI, LO, MID)
K_TERMS = (HI, MID, HI, LO, HI, MID)
TERMS = len(Q_TERMS)
SPLIT = TERMS * HD
BIASED = SPLIT + 3

M_COLS = TILES * NH + 1


def max_items():
    items = []
    for tile in range(TILES):
        keys = P * (tile + 1)
        for part, first, n in ((0, 0, min(keys, 512)), (1, 512, keys - 512)):
            if n > 0:
                heads = {P: 4, 2 * P: 2}.get(n, 1)
                items += [(tile, h, heads, first, n, part) for h in range(0, NH, heads)]
    return items + [(TILES, 0, NH, 0, 512, 0), (TILES, 0, NH, 512, 512, 1), (TILES, 0, NH, 1024, 1, 2)]


Q_CHUNKS = ((0, 384), (384, 768), (768, TP))


def prob_sets():
    return [(c, j, max(lo, P * j), hi - max(lo, P * j))
            for c, (lo, hi) in enumerate(Q_CHUNKS) for j in range(9) if P * j < hi]


MAX_ITEMS = max_items()
SETS = prob_sets()
N_MAX, N_SETS = len(MAX_ITEMS), len(SETS)
LAST_SET = [max(t for t, x in enumerate(SETS) if x[0] == c) for c in range(3)]
RING = 6


def attention_order():
    order, maxima, later, turns = [], 0, [], 0
    for t in range(N_SETS):
        step = later.pop(0) if later else []
        order += [x for x in step if x[0] != "norm"] + [("scores", t)]
        until = min(N_MAX, -(-N_MAX * (t + 1) // (N_SETS - 2)))
        if t:
            order.append(("values", t - 1))
            if t - 1 in LAST_SET:
                c = LAST_SET.index(t - 1)
                order.append(("gather", c))
                later = [[("denominators", c), ("norm", c)], [], [("output", c)]]
        items = [("max", q) for q in range(maxima, until)]
        order += items[:1]
        order += [x for x in step if x[0] == "norm"]
        if not step and t >= 3 and turns < 5:
            order.append(("turn", turns))
            turns += 1
        order += items[1:]
        if maxima < N_MAX == until:
            order.append(("shift", 0))
        elif maxima == N_MAX and ("shift_rows", 0) not in order:
            order.append(("shift_rows", 0))
        maxima = until
    for x in later:
        order += x
    turns_left = [("turn", c) for c in range(turns, 6)]
    return order + [("values", N_SETS - 1), ("gather", 2)] + turns_left + [
        ("denominators", 2), ("project_v", 0), ("norm", 2), ("output", 2)]


ORDER = attention_order()
SHARED_KINDS = ("turn", "shift_rows", "denominators", "output")
SHARED = [x for x in ORDER if x[0] in SHARED_KINDS]
PROLOGUE_SHARED = 3 * 6 + 1


class Image:

    def __init__(self, i, offset):
        self.slot = offset % 2
        self.number = 2 * i + offset
        self.i, self.earlier = i, offset // 2

    def times(self, n, more=0):
        return self.number * n + more

    def of_slot(self, n, more=0):
        return self.i * n + (self.earlier * n + more)


FIRST_IMAGE = Image(0, 0)


def attend(nc, chip, dram, images):
    bank, psum = chip.bank, chip.psum
    dram["parts"] = nc.dram_tensor("scratch_parts", [2, QK, 3, TP], BF16, kind="Internal").ap()
    dram["shift"] = nc.dram_tensor("scratch_shift", [2, 3 * M_COLS, P], BF16, kind="Internal").ap()
    with ExitStack() as ctx:
        counts = []

        def sem(name):
            counts.append(ctx.enter_context(nc.semaphore("a_" + name)))
            return counts[-1]

        def sb(name, cols, dt=F32):
            return ctx.enter_context(nc.sbuf_tensor("a_" + name, [P, cols], dt))

        hn = [sb(f"hn{k}", TP) for k in range(2)]
        z = [sb(f"z{k}", TP) for k in range(2)]
        by_cos, by_sin, qk = sb("by_cos", TP), sb("by_sin", TP), sb("qk", TP)
        rest = sb("rest", TP)
        parts = sb("parts", 3 * TP, BF16)
        flat = [sb(f"split{k}", (NH + NKV) * TP, BF16) for k in range(2)]
        flat_b = [sb(f"biased{k}", (NH + NKV) * TP, BF16) for k in range(2)]
        split = [x[:, :].rearrange("p (h n) -> p h n", h=NH + NKV) for x in flat]
        biased = [x[:, :].rearrange("p (h n) -> p h n", h=NH + NKV) for x in flat_b]
        values = [sb(f"values{k}", 9 * NKV * 32) for k in range(2)]
        v = [x[:, :].rearrange("p (t g c) -> p t g c", t=9, g=NKV) for x in values]
        probs = [sb(f"probs{r}", 2 * 384) for r in range(RING)]
        pr = [x[:, :].rearrange("p (h n) -> p h n", h=2) for x in probs]
        maxima = sb("maxima", 3 * M_COLS)
        mx = maxima[:, :].rearrange("p (a m) -> p a m", a=3)
        shift, shift_rest = sb("shift", M_COLS), sb("shift_rest", M_COLS)
        shift_parts = sb("shift_parts", 3 * M_COLS, BF16)
        sp3 = shift_parts[:, :].rearrange("p (a m) -> p a m", a=3)
        shift_row = sb("shift_row", P, BF16)
        unnormed, recip, y = sb("unnormed", 384), sb("recip", 384), sb("y", 384)
        x2 = sb("x2", TP)

        MAX_BANKS, SCORE_BANKS, SUM_BANK, SHARED_BANK = (0, 1), (2, 4), 6, 7
        v_bank = bank[MAX_BANKS[0]]
        shared, summed = bank[SHARED_BANK], bank[SUM_BANK]

        cleared = sem("cleared")
        hn_loaded = [sem(f"hn_loaded{k}") for k in range(2)]
        z_loaded = [sem(f"z_loaded{k}") for k in range(2)]
        shared_ready = sem("shared_ready")
        shared_read = sem("shared_read")
        v_ready, v_taken = sem("v_ready"), sem("v_taken")
        split_steps = sem("split_steps")
        parts_stored = sem("parts_stored")
        split_loaded = [sem(f"split_loaded{k}") for k in range(2)]
        biased_loaded = [sem(f"biased_loaded{k}") for k in range(2)]
        shift_stored = sem("shift_stored")
        shift_placed = [sem(f"shift_placed{k}") for k in range(2)]
        max_scores = sem("max_scores")
        max_taken = sem("max_taken")
        shift_steps = sem("shift_steps")
        scores = sem("scores")
        exps = sem("exps")
        summed_sets = sem("summed_sets")
        unnormed_ready = sem("unnormed_ready")
        recip_ready = sem("recip_ready")
        y_ready = sem("y_ready")
        x2_stored = sem("x2_stored")
        NSPLIT, NSHIFT, SHIFT_DMAS, N_CLEARED = 5, 5, 2 * 16, 11

        def use(image, step):
            return image.number * len(SHARED) + (PROLOGUE_SHARED + SHARED.index(step) + 1)

        start_counts(nc, counts)
        block = ctx.enter_context(nc.Block())

        def turn_images(i, k):
            return Image(i, k), Image(i, k + 1), Image(i, k + 2), Image(i, k + 3)

        @block.sync
        def _(sp):
            def load_hn(m):
                sp.dma_start(hn[m.slot][0:D, :], bass.AP(dram["hn"].tensor, m.times(D * TP), [[TP, D], [1, TP]]))\
                  .then_inc(hn_loaded[m.slot], 16)

            def load_z(m):
                sp.dma_start(z[m.slot][0:D, :], bass.AP(dram["z"].tensor, m.times(D * TP), [[TP, D], [1, TP]]))\
                  .then_inc(z_loaded[m.slot], 16)

            def lay_out_split(m):
                sp.wait_ge(split_steps, START + m.times(NSPLIT, NSPLIT))
                at = m.slot * (QK * 3 * TP)
                parts_dram = dram["parts"]
                sp.dma_start(bass.AP(parts_dram.tensor, at, [[3 * TP, QK], [1, 3 * TP]]), parts[0:QK, :])\
                  .then_inc(parts_stored, 16)
                sp.wait_ge(parts_stored, START + m.times(16, 16))
                for t in range(TERMS):
                    rows = slice(HD * t, HD * (t + 1))
                    for first, n, term in ((0, NH, Q_TERMS[t]), (NH, NKV, K_TERMS[t])):
                        src = bass.AP(parts_dram.tensor, at + first * HD * 3 * TP + term * TP,
                                      [[3 * TP, HD], [HD * 3 * TP, n], [1, TP]])
                        sp.dma_start(split[m.slot][rows, first:first + n, :], src)\
                          .then_inc(split_loaded[m.slot], 16)

            def copy_biased(m):
                sp.wait_ge(split_loaded[m.slot], START + m.of_slot(16 * 2 * TERMS, 16 * 2 * TERMS))
                sp.dma_start(flat_b[m.slot][0:SPLIT, :], flat[m.slot][0:SPLIT, :])\
                  .then_inc(biased_loaded[m.slot], 16)

            def place_shift(m, taken):
                sp.wait_ge(shared_read, START + taken)
                rows_dram = dram["shift"].tensor
                at = m.slot * (3 * M_COLS * P)
                sp.dma_start(bass.AP(rows_dram, at, [[P, 3 * M_COLS], [1, P]]), shift_row[0:3 * M_COLS, :])\
                  .then_inc(shift_stored, 16)
                sp.wait_ge(shift_stored, START + m.times(16, 16))
                rows = slice(SPLIT, BIASED)
                sp.dma_start(biased[m.slot][rows, 0:NH, 0:L],
                             bass.AP(rows_dram, at, [[M_COLS * P, 3], [L, NH], [1, L]]))\
                  .then_inc(shift_placed[m.slot], 16)
                sp.dma_start(biased[m.slot][rows, 0:NH, L:TP],
                             bass.AP(rows_dram, at + NH * L + 30, [[M_COLS * P, 3], [32, NH], [1, 2]]))\
                  .then_inc(shift_placed[m.slot], 16)

            sp.wait_ge(cleared, START + N_CLEARED)
            first, second = Image(0, 0), Image(0, 1)
            load_hn(first)
            load_hn(second)
            load_z(first)
            sp.wait_ge(v_ready, START + 1)
            load_hn(Image(0, 2))
            lay_out_split(first)
            copy_biased(first)
            lay_out_split(second)
            place_shift(first, PROLOGUE_SHARED)
            with sp.Fori(0, images // 2) as i:
                for k in range(2):
                    now, soon, later, last = turn_images(i, k)
                    sp.wait_ge(shared_read, START + now.times(len(SHARED), PROLOGUE_SHARED))
                    load_z(soon)
                    load_hn(last)
                    copy_biased(soon)
                    sp.wait_ge(max_scores, START + soon.times(N_MAX))
                    sp.wait_ge(biased_loaded[later.slot], START + later.of_slot(16))
                    lay_out_split(later)
                    place_shift(soon, use(now, ("shift_rows", 0)))
                    sp.wait_ge(shared_read, START + use(now, ("output", 2)))
                    sp.dma_start(bass.AP(dram["x2"].tensor, now.times(D * TP), [[TP, D], [1, TP]]), x2[0:D, :])\
                      .then_inc(x2_stored, 16)
            sp.wait_ge(x2_stored, START + 16 * images)
            for k in range(2):
                n = images // 2
                sp.wait_ge(hn_loaded[k], START + 16 * (n + 2 - k))
                sp.wait_ge(split_loaded[k], START + (n + 1) * (16 * 2 * TERMS))
                for fetched, by in ((z_loaded, 16), (biased_loaded, 16), (shift_placed, SHIFT_DMAS)):
                    sp.wait_ge(fetched[k], START + by * (n + 1 - k))

        @block.gpsimd
        def _(pool):
            for k in range(2):
                pool.memset(values[k][:, 0:TILES * NKV * 32], 1.0).then_inc(cleared, 1)
                pool.memset(values[k][:, TILES * NKV * 32:], 0.0).then_inc(cleared, 1)
            pool.memset(maxima[:, :], -3e38).then_inc(cleared, 1)
            pool.wait_ge(cleared, START + N_CLEARED - 2)
            for k in range(2):
                pool.memset(values[k][0:1, TILES * NKV * 32:], 1.0).then_inc(cleared, 1)
            pool.wait_ge(cleared, START + N_CLEARED)

            def split_up(m, turned):
                p3 = parts[0:QK, :].rearrange("p (a n) -> p a n", a=3)
                step = m.times(NSPLIT)
                pool.wait_ge(shared_read, START + turned)
                pool.tensor_tensor(qk[0:QK, :], by_cos[0:QK, :], by_sin[0:QK, :], ALU.add).then_inc(split_steps, 1)
                pool.wait_ge(parts_stored, START + m.times(16))
                pool.tensor_tensor(p3[:, HI, :], by_cos[0:QK, :], by_sin[0:QK, :], ALU.add).then_inc(split_steps, 1)
                pool.wait_ge(split_steps, START + step + 2)
                pool.tensor_tensor(rest[0:QK, :], qk[0:QK, :], p3[:, HI, :], ALU.subtract).then_inc(split_steps, 1)
                pool.tensor_tensor(p3[:, MID, :], qk[0:QK, :], p3[:, HI, :], ALU.subtract).then_inc(split_steps, 1)
                pool.wait_ge(split_steps, START + step + 4)
                pool.tensor_tensor(p3[:, LO, :], rest[0:QK, :], p3[:, MID, :], ALU.subtract).then_inc(split_steps, 1)

            split_up(Image(0, 0), 6)
            split_up(Image(0, 1), 12)
            with pool.Fori(0, images // 2) as i:
                for k in range(2):
                    now, _, later, _ = turn_images(i, k)
                    split_up(later, now.times(len(SHARED), PROLOGUE_SHARED))

        @block.scalar
        def _(act):
            act.wait_ge(cleared, START + N_CLEARED)

            def take_v(m):
                act.wait_ge(v_ready, START + m.times(1, 1))
                got = v_bank[:, 0:9 * NKV * HD].rearrange("p (t g c) -> p t g c", t=9, g=NKV)
                act.activation(v[m.slot][:, 0:8, :, 0:HD].rearrange("p t g c -> p (t g) c"),
                               got[:, 0:8].rearrange("p t g c -> p (t g) c"), ACT.Copy)
                act.activation(v[m.slot][0:1, 8, :, 0:HD], got[0:1, 8], ACT.Copy).then_inc(v_taken, 1)

            def take_row(m, at):
                act.wait_ge(shared_ready, START + at)
                act.activation(shift_row[0:3 * M_COLS, :], shared[:, :].bitcast(BF16)[0:3 * M_COLS, 0:P], ACT.Copy)\
                   .then_inc(shared_read, 1)

            take_v(Image(0, 0))
            take_v(Image(0, 1))
            take_row(Image(0, 0), PROLOGUE_SHARED)
            with act.Fori(0, images // 2) as i:
                for k in range(2):
                    now, soon, later, _ = turn_images(i, k)
                    for kind, x in ORDER:
                        if kind == "scores":
                            c, j, first, n = SETS[x]
                            keys = P if j < TILES else 1
                            act.wait_ge(summed_sets, START + now.times(N_SETS, max(x - RING // 2 + 1, 0)))
                            for half in range(2):
                                act.wait_ge(scores, START + now.times(2 * N_SETS, 2 * x + half + 1))
                                b = SCORE_BANKS[half]
                                act.activation(pr[(2 * x + half) % RING][0:keys, :, 0:n],
                                               psum[0:keys, b:b + 2, 0:n], ACT.Exp, scale=HD ** -0.5)\
                                   .then_inc(exps, 1)
                        elif kind == "gather":
                            w = Q_CHUNKS[x][1] - Q_CHUNKS[x][0]
                            act.wait_ge(summed_sets, START + now.times(N_SETS, LAST_SET[x] + 1))
                            act.wait_ge(y_ready, START + now.times(3, x))
                            act.activation(unnormed[:, 0:w], summed[:, 0:w], ACT.Copy).then_inc(unnormed_ready, 1)
                        elif kind == "project_v":
                            act.wait_ge(summed_sets, START + now.times(N_SETS, N_SETS))
                            take_v(later)
                        elif kind == "shift_rows":
                            act.wait_ge(shift_placed[now.slot], START + now.of_slot(SHIFT_DMAS, SHIFT_DMAS))
                            take_row(soon, use(now, (kind, x)))

        @block.vector
        def _(dve):
            for k in range(2):
                dve.memset(hn[k][D:P, :], 0.0).then_inc(cleared, 1)
                dve.memset(flat_b[k][SPLIT:P, NH * TP:], 1.0).then_inc(cleared, 1)
            dve.wait_ge(cleared, START + N_CLEARED)

            def take_turn(m, c, at):
                third, swapped = divmod(c, 2)
                to, table = (by_sin, C_SIN) if swapped else (by_cos, C_COS)
                cols = slice(third * THIRD, (third + 1) * THIRD)
                dve.wait_ge(shared_ready, START + at)
                dve.tensor_tensor(to[0:QK, cols], shared[0:QK, 0:THIRD], chip.const(table, TP)[0:QK, cols], ALU.mult)\
                   .then_inc(shared_read, 1)

            def take_max(m, q):
                tile, h, heads, _, n, part = MAX_ITEMS[q]
                dve.wait_ge(max_scores, START + m.times(N_MAX, q + 1))
                b = MAX_BANKS[(m.slot * N_MAX + q) % 2]
                if tile < TILES:
                    got = bank[b][:, 0:heads * n].rearrange("p (h n) -> p h n", h=heads)
                    col = h * TILES + tile
                    to = mx[:, part, col:col + (heads - 1) * TILES + 1:TILES]
                else:
                    got, to = bank[b][:, 0:n], mx[:, part, M_COLS - 1:M_COLS]
                dve.tensor_reduce(to, got, AX_X, ALU.max).then_inc(max_taken, 1)

            def split_shift(m):
                step = m.times(NSHIFT)
                dve.wait_ge(max_taken, START + m.times(N_MAX, N_MAX))
                dve.tensor_reduce(shift[:, :], mx.rearrange("p a m -> p m a"), AX_X, ALU.max)\
                   .then_inc(shift_steps, 1)
                dve.wait_ge(shift_steps, START + step + 1)
                dve.tensor_scalar(sp3[:, HI, :], shift[:, :], -1.0, None, ALU.mult).then_inc(shift_steps, 1)
                dve.wait_ge(shift_steps, START + step + 2)
                dve.scalar_tensor_tensor(shift_rest[:, :], shift[:, :], -1.0, sp3[:, HI, :], ALU.mult, ALU.subtract)\
                   .then_inc(shift_steps, 1)
                dve.wait_ge(shift_steps, START + step + 3)
                dve.tensor_copy(sp3[:, MID, :], shift_rest[:, :]).then_inc(shift_steps, 1)
                dve.wait_ge(shift_steps, START + step + 4)
                dve.tensor_tensor(sp3[:, LO, :], shift_rest[:, :], sp3[:, MID, :], ALU.subtract)\
                   .then_inc(shift_steps, 1)

            for n in range(3):
                for c in range(6):
                    if n > 0 and c == 0:
                        dve.wait_ge(split_steps, START + (n - 1) * NSPLIT + 2)
                    take_turn(Image(0, n), c, n * 6 + c + 1)
            for q in range(N_MAX):
                take_max(Image(0, 0), q)
            split_shift(Image(0, 0))
            with dve.Fori(0, images // 2) as i:
                for k in range(2):
                    now, soon, later, last = turn_images(i, k)
                    for kind, x in ORDER:
                        if kind == "turn":
                            if x == 0:
                                dve.wait_ge(split_steps, START + later.times(NSPLIT, 2))
                            take_turn(last, x, use(now, (kind, x)))
                        elif kind == "max":
                            take_max(soon, x)
                        elif kind == "shift":
                            split_shift(soon)
                        elif kind == "denominators":
                            w = Q_CHUNKS[x][1] - Q_CHUNKS[x][0]
                            dve.wait_ge(shared_ready, START + use(now, (kind, x)))
                            dve.wait_ge(y_ready, START + now.times(3, x))
                            dve.reciprocal(recip[:, 0:w // 2], shared[:, 0:w // 2]).then_inc(recip_ready, 1)
                        elif kind == "norm":
                            w = Q_CHUNKS[x][1] - Q_CHUNKS[x][0]
                            dve.reciprocal(recip[:, w // 2:w], shared[:, w // 2:w]).then_inc(shared_read, 1)
                            dve.wait_ge(shared_read, START + use(now, ("denominators", x)))
                            dve.wait_ge(recip_ready, START + now.times(3, x + 1))
                            dve.wait_ge(unnormed_ready, START + now.times(3, x + 1))
                            dve.tensor_tensor(y[:, 0:w], unnormed[:, 0:w], recip[:, 0:w], ALU.mult)\
                               .then_inc(y_ready, 1)
                        elif kind == "output":
                            lo, hi = Q_CHUNKS[x]
                            dve.wait_ge(shared_ready, START + use(now, (kind, x)))
                            if x == 0:
                                dve.wait_ge(z_loaded[now.slot], START + now.of_slot(16, 16))
                                dve.wait_ge(x2_stored, START + now.times(16))
                            dve.tensor_tensor(x2[0:D, lo:hi], z[now.slot][0:D, lo:hi], shared[0:D, 0:hi - lo], ALU.add)\
                               .then_inc(shared_read, 1)

        @block.tensor
        def _(pe):
            pe.wait_ge(cleared, START + N_CLEARED)

            def turn(m, c, at):
                third, swapped = divmod(c, 2)
                if c == 0:
                    pe.wait_ge(hn_loaded[m.slot], START + m.of_slot(16, 16))
                pe.wait_ge(shared_read, START + at - 1)
                pe.matmul(shared[0:QK, 0:THIRD], (chip.qk_swapped if swapped else chip.qk_w)[:, :],
                          hn[m.slot][:, third * THIRD:(third + 1) * THIRD], start=True, stop=True)\
                  .then_inc(shared_ready, 1)

            def project_v(m):
                pe.wait_ge(v_taken, START + m.number)
                n = NKV * HD
                for t in range(9):
                    keys = P if t < TILES else 2
                    ins = pe.matmul(v_bank[0:keys, t * n:(t + 1) * n], hn[m.slot][:, t * P:t * P + keys],
                                    chip.v_w[:, :], start=True, stop=True)
                ins.then_inc(v_ready, 1)

            def score_for_max(m, q):
                tile, h, heads, first, n, _ = MAX_ITEMS[q]
                x = split[m.slot]
                if q == 0:
                    pe.wait_ge(split_loaded[m.slot], START + m.of_slot(16 * 2 * TERMS, 16 * 2 * TERMS))
                if q < 2:
                    pe.wait_ge(v_taken, START + m.times(1, 2 if m is FIRST_IMAGE else 1))
                if m is not FIRST_IMAGE or q >= 2:
                    pe.wait_ge(max_taken, START + m.times(N_MAX, q - 1))
                b = MAX_BANKS[(m.slot * N_MAX + q) % 2]
                if tile == TILES:
                    for a in range(NH):
                        ins = pe.matmul(bank[b][32 * a:32 * (a + 1), 0:n], x[0:SPLIT, a, TP - 32:TP],
                                        x[0:SPLIT, NH + a // 2, first:first + n], start=True, stop=True)
                else:
                    diagonal = first + n == P * (tile + 1)
                    for a in range(heads):
                        ins = pe.matmul(bank[b][:, a * n:(a + 1) * n], x[0:SPLIT, h + a, P * tile:P * (tile + 1)],
                                        x[0:SPLIT, NH + (h + a) // 2, first:first + n],
                                        start=True, stop=not diagonal)
                        if diagonal:
                            ins = pe.matmul(bank[b][:, (a + 1) * n - P:(a + 1) * n], chip.ident16[:, :],
                                            chip.mask_q16[:, :], start=False, stop=True)
                ins.then_inc(max_scores, 1)

            def turn_shift(m, at):
                pe.wait_ge(shift_steps, START + m.times(NSHIFT, NSHIFT))
                pe.wait_ge(shared_read, START + at - 1)
                pe.transpose(shared[:, :].bitcast(BF16)[0:3 * M_COLS, 0:P], shift_parts[:, :], chip.ident16[:, :])\
                  .then_inc(shared_ready, 1)

            def score(m, t):
                c, j, first, n = SETS[t]
                keys = P if j < TILES else 1
                x = biased[m.slot]
                if t == 0:
                    pe.wait_ge(biased_loaded[m.slot], START + m.of_slot(16, 16))
                    pe.wait_ge(shift_placed[m.slot], START + m.of_slot(SHIFT_DMAS, SHIFT_DMAS))
                masked = P * j >= Q_CHUNKS[c][0] and j < TILES
                for half in range(2):
                    pe.wait_ge(exps, START + m.times(2 * N_SETS, max(2 * t + half - 1, 0)))
                    for a in range(2):
                        b = SCORE_BANKS[half] + a
                        ins = pe.matmul(bank[b][0:keys, 0:n], x[0:BIASED, NH + half, P * j:P * j + keys],
                                        x[0:BIASED, 2 * half + a, first:first + n], start=True, stop=not masked)
                        if masked:
                            ins = pe.matmul(bank[b][:, 0:P], chip.ident16[:, :], chip.mask_k16[:, :],
                                            start=False, stop=True)
                    ins.then_inc(scores, 1)

            def weigh_values(m, t):
                c, j, first, n = SETS[t]
                lo, hi = Q_CHUNKS[c]
                if j == 0:
                    pe.wait_ge(unnormed_ready, START + m.times(3, c))
                last = t in LAST_SET
                for h in range(NH):
                    if h % 2 == 0:
                        pe.wait_ge(exps, START + m.times(2 * N_SETS, 2 * t + h // 2 + 1))
                    ins = pe.matmul(summed[32 * h:32 * (h + 1), first - lo:hi - lo],
                                    v[m.slot][:, j, h // 2, :],
                                    pr[(2 * t + h // 2) % RING][:, h % 2, 0:n], start=j == 0, stop=last)
                ins.then_inc(summed_sets, 1)

            for n in range(3):
                for c in range(6):
                    turn(Image(0, n), c, n * 6 + c + 1)
                if n < 2:
                    project_v(Image(0, n))
            for q in range(N_MAX):
                score_for_max(FIRST_IMAGE, q)
            turn_shift(Image(0, 0), PROLOGUE_SHARED)
            with pe.Fori(0, images // 2) as i:
                for k in range(2):
                    now, soon, later, last = turn_images(i, k)
                    for kind, x in ORDER:
                        at = use(now, (kind, x)) if kind in SHARED_KINDS else None
                        if kind == "scores":
                            score(now, x)
                        elif kind == "values":
                            weigh_values(now, x)
                        elif kind == "max":
                            score_for_max(soon, x)
                        elif kind == "turn":
                            turn(last, x, at)
                        elif kind == "project_v":
                            pe.wait_ge(max_taken, START + soon.times(N_MAX, N_MAX))
                            project_v(later)
                        elif kind == "shift_rows":
                            turn_shift(soon, at)
                        elif kind == "denominators":
                            w = Q_CHUNKS[x][1] - Q_CHUNKS[x][0]
                            pe.wait_ge(unnormed_ready, START + now.times(3, x + 1))
                            pe.wait_ge(shared_read, START + at - 1)
                            pe.matmul(shared[:, 0:w], chip.const(C_DEN), unnormed[:, 0:w], start=True, stop=True)\
                              .then_inc(shared_ready, 1)
                        elif kind == "output":
                            w = Q_CHUNKS[x][1] - Q_CHUNKS[x][0]
                            pe.wait_ge(y_ready, START + now.times(3, x + 1))
                            pe.wait_ge(shared_read, START + at - 1)
                            pe.matmul(shared[0:D, 0:w], chip.o_w[:, :], y[:, 0:w], start=True, stop=True)\
                              .then_inc(shared_ready, 1)



UNITS = 3 * 2 * PAIRS * 3
GROUPS = UNITS // 3
LAG = 2
FOLDS = GROUPS // PAIRS
ADDS = PAIRS - 1
EMIT_TILES = (range(0, 2), range(2, 5), range(5, 9))
HIDDEN_RING = 4


CHOICES = 13
CHOSEN = 2 * CHOICES - 1


def experts_order():
    ahead = {5: ("square", 0), 8: ("mean", 0), 9: ("mean", 1), 10: ("mean", 2), 11: ("norm", 0), 14: ("split", 0),
             15: ("split", 1), 17: ("route", 0), 18: ("choose", 0), 31: ("exponents", 0)}
    ahead.update({33 + x: ("choose", x) for x in range(1, CHOICES)})
    order, later = [], {}
    for u in range(LAG, UNITS + LAG):
        if (u - LAG) % 3 == 0:
            order.append(("spread", (u - LAG) // 3))
        order += [("up", u), ("down", u - LAG)]
        if (u - LAG) % 3 == 2:
            order.append(("weigh", (u - LAG) // 3))
        if u > LAG + 1 and (u - LAG - 1) % (3 * PAIRS) == 0:
            f = (u - LAG - 1) // (3 * PAIRS) - 1
            order.append(("fold", f))
            if f % 2 == 1:
                order.append(("close", f // 2))
                later[u + 2] = ("emit", f // 2)
        order += [x[u] for x in (later, ahead) if u in x]
    return order + [("turn_weights", 0), ("fold", FOLDS - 1), ("close", 2), ("turn_weights", 1), ("emit", 2)]


E_ORDER = experts_order()
E_SHARED_KINDS = ("spread", "mean", "route", "turn_weights", "emit")
E_SHARED = [x for x in E_ORDER if x[0] in E_SHARED_KINDS]
E_PROLOGUE = [("square", 0), ("mean", 0), ("mean", 1), ("mean", 2), ("norm", 0), ("split", 0),
              ("split", 1), ("route", 0), ("choose", 0), ("exponents", 0)]
E_PROLOGUE += [("choose", x) for x in range(1, CHOICES)]
E_PROLOGUE += [("turn_weights", 0), ("turn_weights", 1)]
E_PROLOGUE_SHARED = [x for x in E_PROLOGUE if x[0] in E_SHARED_KINDS]


def route_and_mix_experts(nc, chip, dram, images):
    bank = chip.bank
    turns = images // 4
    A_BANKS, B_BANKS, OUT_BANKS, SUM_BANK, SHARED_BANK = (0, 1), (2, 3), (4, 5), 6, 7
    shared, total = bank[SHARED_BANK], bank[SUM_BANK]
    GR = 9 * 2
    with ExitStack() as ctx:
        counts = []

        def sem(name):
            counts.append(ctx.enter_context(nc.semaphore("e_" + name)))
            return counts[-1]

        def sb(name, cols, dt=F32):
            return ctx.enter_context(nc.sbuf_tensor("e_" + name, [P, cols], dt))

        x2 = [sb(f"x2{k}", TP) for k in range(2)]
        h2 = [sb(f"h2{k}", TP) for k in range(2)]
        base = [sb(f"base{k}", TP) for k in range(2)]
        flat = sb("flat", TP)
        high, low = sb("high", TP, F16), sb("low", TP, F16)
        halves = [[sb(f"halves{k}{b}", TP, F16) for b in range(2)] for k in range(2)]
        turned = [sb(f"turned{k}", 9 * P, BF16) for k in range(2)]
        squares, rms = sb("squares", TP), sb("rms", TP)
        gate = [sb(f"gate{r}", THIRD) for r in range(HIDDEN_RING)]
        hidden = [sb(f"hidden{r}", THIRD) for r in range(HIDDEN_RING)]
        spread = [sb(f"spread{r}", THIRD) for r in range(2)]
        weighed = [sb(f"weighed{r}", THIRD) for r in range(2)]
        added = [sb(f"added{r}", THIRD) for r in range(2)]
        whole = sb("whole", TP)
        outs = [sb(f"outs{r}", 4 * P) for r in range(2)]
        logit, prob, one_hot, second, other = (sb(n, GR * NE) for n in ("logit", "prob", "one_hot", "second", "other"))
        best, best2, per_group = sb("best", GR), sb("best2", GR), sb("per_group", GR)
        wparts = sb("wparts", 9 * 96, BF16)

        cleared = sem("cleared")
        loaded = [sem(f"loaded{k}") for k in range(2)]
        stored = [sem(f"stored{k}") for k in range(2)]
        shared_ready, shared_read = sem("shared_ready"), sem("shared_read")
        squared = sem("squared")
        based = sem("based")
        rms_ready = sem("rms_ready")
        flat_ready = sem("flat_ready")
        moved = sem("moved")
        chosen = sem("chosen")
        exp_ready = sem("exp_ready")
        up_a, up_b = sem("up_a"), sem("up_b")
        gates, hiddens = sem("gates"), sem("hiddens")
        downs = sem("downs")
        weighs, adds = sem("weighs"), sem("adds")
        folds, closes = sem("folds"), sem("closes")

        def use(n, step):
            return n * len(E_SHARED) + (len(E_PROLOGUE_SHARED) + E_SHARED.index(step) + 1)

        def use_first(step):
            return E_PROLOGUE_SHARED.index(step) + 1

        def rows(name, pair):
            return bass.AP(dram[name].tensor, pair * (2 * D * TP), [[TP, P], [1, TP]])

        def groups(ap):
            return ap[:, :].rearrange("p (g e) -> p g e", e=NE)

        def to_all(ap):
            return bass.AP(ap, 0, [[GR, P], [1, GR], [0, NE]])

        def third(ap, c):
            return ap[:, c * THIRD:(c + 1) * THIRD]

        def unit(u):
            return u // (2 * PAIRS * 3), u // (PAIRS * 3) % 2, u // 3 % PAIRS, u % 3

        EMITTED = [sum((2 + (x == 2)) for s in range(2) for x in range(3) if (s + x) % 2 == k) for k in range(2)]

        def emitted_before(i, k, x):
            r = (k + x) % 2
            inside = sum((2 + (xx == 2)) for s in range(2) for xx in range(3)
                         if (s + xx) % 2 == r and (s, xx) < (k, x))
            return i * (16 * EMITTED[r]) + 16 * inside

        start_counts(nc, counts)
        block = ctx.enter_context(nc.Block())

        @block.sync
        def _(sp):
            def load(n, slot):
                sp.dma_start(x2[slot][:, :], rows("x2", n)).then_inc(loaded[slot], 16)
                sp.dma_start(h2[slot][:, :], rows("h2", n)).then_inc(loaded[slot], 16)

            def emit(n, slot, x):
                sp.wait_ge(shared_read, START + use(n, ("emit", x)))
                tiles = [t for t in EMIT_TILES[x] if t < TILES]
                r = outs[(slot + x) % 2]
                for b in range(2):
                    src = r[:, 0:len(tiles) * P].rearrange("p (t u d) -> p t u d", u=2, d=D)[:, :, b, :]
                    to = bass.AP(dram["out"].tensor, (2 * n + b) * (T * D) + tiles[0] * P * D,
                                 [[D, P], [P * D, len(tiles)], [1, D]])
                    sp.dma_start(to, src).then_inc(stored[(slot + x) % 2], 16)
                if x == 2:
                    sp.dma_start(bass.AP(dram["out"].tensor, 2 * n * (T * D) + L * D, [[0, 1], [T * D, 2], [1, D]]),
                                 r[0:1, 3 * P:4 * P].rearrange("p (u d) -> p u d", u=2))\
                      .then_inc(stored[(slot + x) % 2], 16)

            def move(n, slot):
                for b in range(2):
                    for part, source in enumerate((high, low)):
                        sp.dma_start(halves[slot][b][D * part:D * (part + 1), :], source[D * b:D * (b + 1), :])\
                          .then_inc(moved, 16)

            load(0, 0)
            sp.wait_ge(flat_ready, START + 3)
            move(0, 0)
            with sp.Fori(0, turns) as i:
                for k in range(2):
                    n = sp.snap(2 * i + k)
                    sp.wait_ge(closes, START + n * 3)
                    load(n + 1, (k + 1) % 2)
                    emit(n, k, 0)
                    sp.wait_ge(flat_ready, START + n * 3 + 6)
                    move(n + 1, (k + 1) % 2)
                    emit(n, k, 1)
                    emit(n, k, 2)
            for k in range(2):
                sp.wait_ge(stored[k], START + 16 * EMITTED[k] * turns)
                sp.wait_ge(loaded[k], START + 32 * (turns + 1 - k))

        @block.gpsimd
        def _(pool):
            pool.memset(wparts[:, :], 0.0).then_inc(cleared, 1)

            pool.wait_ge(loaded[0], START + 32)
            pool.tensor_tensor(base[0][:, :], x2[0][:, :], h2[0][:, :], ALU.add).then_inc(based, 1)
            with pool.Fori(0, turns) as i:
                for k in range(2):
                    n = pool.snap(2 * i + k)
                    for f in range(FOLDS):
                        to = added[f % 2]
                        for p in range(1, PAIRS):
                            g = f * PAIRS + p
                            pool.wait_ge(weighs, START + n * GROUPS + (g + 1))
                            if p == 1:
                                pool.wait_ge(folds, START + n * FOLDS + max(f - 1, 0))
                            else:
                                pool.wait_ge(adds, START + n * (ADDS * FOLDS) + (f * ADDS + p - 1))
                            pool.tensor_tensor(to[:, :], (weighed[(g - 1) % 2] if p == 1 else to)[:, :],
                                               weighed[g % 2][:, :], ALU.add).then_inc(adds, 1)
                        if f == 0:
                            pool.wait_ge(closes, START + n * 3)
                            pool.wait_ge(loaded[(k + 1) % 2], START + (i + 1 + k) * 32)
                            s = (k + 1) % 2
                            pool.tensor_tensor(base[s][:, :], x2[s][:, :], h2[s][:, :], ALU.add).then_inc(based, 1)

        @block.scalar
        def _(act):
            act.wait_ge(cleared, START + 1)

            def step(kind, x, n, k, slot, at, pair):
                if kind == "square":
                    act.wait_ge(loaded[slot], START + pair[1] * 32)
                    act.activation(squares[:, :], x2[slot][:, :], ACT.Square).then_inc(squared, 1)
                elif kind == "norm":
                    act.wait_ge(shared_read, START + at)
                    act.activation(rms[:, :], rms[:, :], ACT.Ln, bias=chip.v("rms_eps")).then_inc(rms_ready, 1)
                    act.wait_ge(rms_ready, START + pair[0] * 2 + 1)
                    act.activation(rms[:, :], rms[:, :], ACT.Exp, scale=-0.5).then_inc(rms_ready, 1)
                elif kind == "exponents":
                    act.wait_ge(shared_read, START + at)
                    act.activation(prob[:, :], logit[:, :], ACT.Exp).then_inc(exp_ready, 1)
                elif kind == "turn_weights":
                    act.wait_ge(shared_ready, START + at)
                    got = shared[:, :].bitcast(BF16)
                    if x == 0:
                        act.activation(turned[slot][0:96, 0:L], got[0:96, 0:L], ACT.Copy).then_inc(shared_read, 1)
                    else:
                        act.activation(turned[slot][0:96, L:TP], got[0:96, P - 2:P], ACT.Copy)\
                           .then_inc(shared_read, 1)

            def take_gate(n, x):
                r = x % HIDDEN_RING
                n_rows = CHUNKS[x % 3][1]
                act.wait_ge(up_a, START + n * UNITS + (x + 1))
                if x >= LAG:
                    act.wait_ge(hiddens, START + n * UNITS + max(x - HIDDEN_RING + 1, 0))
                act.activation(gate[r][0:n_rows, :], bank[A_BANKS[x % 2]][0:n_rows, 0:THIRD], ACT.Silu,
                               scale=chip.unscale[0:n_rows, 0:1]).then_inc(gates, 1)

            source = {"norm": ("mean", 2), "exponents": ("route", 0)}
            for kind, x in E_PROLOGUE:
                if kind not in ("square", "norm", "exponents", "turn_weights"):
                    continue
                at = use_first(source.get(kind, (kind, x))) if kind != "square" else None
                step(kind, x, 0, 0, 0, at, (0, 1))
            for x in range(LAG):
                take_gate(0, x)
            with act.Fori(0, turns) as i:
                for k in range(2):
                    n = act.snap(2 * i + k)
                    for kind, x in E_ORDER:
                        if kind == "up":
                            take_gate(n, x)
                        elif kind == "spread":
                            act.wait_ge(shared_ready, START + use(n, (kind, x)))
                            act.wait_ge(weighs, START + n * GROUPS + max(x - 1, 0))
                            act.activation(spread[x % 2][:, :], shared[:, 0:THIRD], ACT.Copy).then_inc(shared_read, 1)
                        elif kind in ("square", "norm", "exponents", "turn_weights"):
                            at = use(n, source.get(kind, (kind, x))) if kind != "square" else None
                            step(kind, x, n, k, (k + 1) % 2, at, (n + 1, i + 1 + k))

        @block.vector
        def _(dve):
            dve.wait_ge(cleared, START + 1)

            first_weight = groups(chip.const(C_FIRST, GR * NE))
            lg, pb, oh, sc, ot = (groups(x) for x in (logit, prob, one_hot, second, other))
            parts = wparts[:, :].rearrange("p (t a r) -> p t a r", t=9, a=3)
            w = prob[:, :].rearrange("p (t r) -> p t r", t=9)
            left = second[:, :].rearrange("p (t r) -> p t r", t=9)

            def choose(pair, x, at):
                before = pair * CHOSEN + max(2 * x - 1, 0)

                def then(ins, n=1):
                    ins.then_inc(chosen, 1)
                    if n == 1 and x > 0:
                        dve.wait_ge(chosen, START + before + 1)

                if x == 0:
                    raw = shared[:, 0:GR * NE].rearrange("p (g e) -> p g e", e=NE)
                    dve.wait_ge(shared_ready, START + at)
                    then(dve.tensor_reduce(best[:, :], raw, AX_X, ALU.max))
                    dve.wait_ge(chosen, START + before + 1)
                    dve.wait_ge(exp_ready, START + pair)
                    dve.tensor_tensor(lg, raw, to_all(best), ALU.subtract).then_inc(shared_read, 1)
                    return
                dve.wait_ge(chosen, START + before)
                if x == 1:
                    dve.wait_ge(exp_ready, START + pair + 1)
                    then(dve.tensor_reduce(per_group[:, :], pb, AX_X, ALU.add))
                    then(dve.reciprocal(per_group[:, :], per_group[:, :]), 2)
                elif x == 2:
                    then(dve.tensor_tensor(pb, pb, to_all(per_group), ALU.mult))
                    then(dve.tensor_reduce(best[:, :], pb, AX_X, ALU.max), 2)
                elif x == 3:
                    then(dve.tensor_tensor(oh, pb, to_all(best), ALU.is_equal))
                    then(dve.tensor_tensor(oh, oh, first_weight, ALU.mult), 2)
                elif x == 4:
                    then(dve.tensor_reduce(per_group[:, :], oh, AX_X, ALU.max))
                    then(dve.tensor_tensor(oh, oh, to_all(per_group), ALU.is_equal), 2)
                elif x == 5:
                    then(dve.scalar_tensor_tensor(second[:, :], one_hot[:, :], -2.0, prob[:, :], ALU.mult, ALU.add))
                    then(dve.tensor_reduce(best2[:, :], sc, AX_X, ALU.max), 2)
                elif x == 6:
                    then(dve.tensor_tensor(ot, sc, to_all(best2), ALU.is_equal))
                    then(dve.tensor_tensor(ot, ot, first_weight, ALU.mult), 2)
                elif x == 7:
                    then(dve.tensor_reduce(per_group[:, :], ot, AX_X, ALU.max))
                    then(dve.tensor_tensor(ot, ot, to_all(per_group), ALU.is_equal), 2)
                elif x == 8:
                    then(dve.tensor_tensor(oh, oh, ot, ALU.add))
                    then(dve.tensor_tensor(pb, pb, oh, ALU.mult), 2)
                elif x == 9:
                    then(dve.scalar_tensor_tensor(per_group[:, :], best[:, :], 1e-9, best2[:, :], ALU.add, ALU.add))
                    then(dve.reciprocal(per_group[:, :], per_group[:, :]), 2)
                elif x == 10:
                    then(dve.tensor_tensor(pb, pb, to_all(per_group), ALU.mult))
                    then(dve.tensor_copy(parts[:, :, 0, 0:16], w), 2)
                elif x == 11:
                    then(dve.tensor_tensor(left, w, parts[:, :, 0, 0:16], ALU.subtract))
                    then(dve.tensor_copy(parts[:, :, 1, 0:16], left), 2)
                else:
                    then(dve.tensor_tensor(left, left, parts[:, :, 1, 0:16], ALU.subtract))
                    then(dve.tensor_copy(parts[:, :, 2, 0:16], left), 2)

            def prepare(kind, x, pair, slot, at):
                if kind == "mean":
                    dve.wait_ge(shared_ready, START + at)
                    if x == 0:
                        dve.wait_ge(flat_ready, START + pair * 3)
                    dve.tensor_copy(third(rms, x), shared[:, 0:THIRD]).then_inc(shared_read, 1)
                elif kind == "norm":
                    dve.wait_ge(rms_ready, START + pair * 2 + 2)
                    dve.tensor_tensor(flat[:, :], x2[slot][:, :], rms[:, :], ALU.mult).then_inc(flat_ready, 1)
                elif x == 0:
                    dve.wait_ge(moved, START + pair * 64)
                    dve.scalar_tensor_tensor(high[:, :], x2[slot][:, :], X_SCALE, rms[:, :], ALU.mult, ALU.mult)\
                       .then_inc(flat_ready, 1)
                else:
                    dve.wait_ge(flat_ready, START + pair * 3 + 2)
                    dve.scalar_tensor_tensor(low[:, :], flat[:, :], X_SCALE, high[:, :], ALU.mult, ALU.subtract)\
                       .then_inc(flat_ready, 1)

            for kind, x in E_PROLOGUE:
                if kind in ("mean", "norm", "split"):
                    prepare(kind, x, 0, 0, use_first((kind, x)) if kind == "mean" else None)
            def hide(n, x):
                r = x % HIDDEN_RING
                n_rows = CHUNKS[x % 3][1]
                dve.wait_ge(up_b, START + n * UNITS + (x + 1))
                dve.wait_ge(gates, START + n * UNITS + (x + 1))
                if x >= LAG:
                    dve.wait_ge(downs, START + n * UNITS + max(x - HIDDEN_RING + 1, 0))
                dve.scalar_tensor_tensor(hidden[r][0:n_rows, :], bank[B_BANKS[x % 2]][0:n_rows, 0:THIRD],
                                         chip.unscale[0:n_rows, 1:2], gate[r][0:n_rows, :],
                                         ALU.mult, ALU.mult).then_inc(hiddens, 1)

            for x in range(CHOICES):
                choose(0, x, use_first(("route", 0)))
            for x in range(LAG):
                hide(0, x)
            with dve.Fori(0, turns) as i:
                for k in range(2):
                    n = dve.snap(2 * i + k)
                    for kind, x in E_ORDER:
                        if kind == "up":
                            hide(n, x)
                        elif kind == "weigh":
                            dve.wait_ge(downs, START + n * UNITS + 3 * (x + 1))
                            dve.wait_ge(shared_read, START + use(n, ("spread", x)))
                            before = max(x - 2, 0)
                            taken = before // PAIRS * ADDS + max(before % PAIRS, 1) if x >= 2 else 0
                            dve.wait_ge(adds, START + n * (ADDS * FOLDS) + taken)
                            dve.tensor_tensor(weighed[x % 2][:, :], bank[OUT_BANKS[x % 2]][:, 0:THIRD],
                                              spread[x % 2][:, :], ALU.mult).then_inc(weighs, 1)
                        elif kind == "close":
                            dve.wait_ge(folds, START + n * FOLDS + 2 * (x + 1))
                            dve.wait_ge(based, START + n + 1)
                            dve.tensor_tensor(third(whole, x), third(base[k], x), total[:, 0:THIRD], ALU.add)\
                               .then_inc(closes, 1)
                        elif kind == "emit":
                            r = (k + x) % 2
                            dve.wait_ge(shared_ready, START + use(n, (kind, x)))
                            dve.wait_ge(stored[r], START + emitted_before(i, k, x))
                            full = len([t for t in EMIT_TILES[x] if t < TILES]) * P
                            if x == 2:
                                dve.tensor_copy(outs[r][0:1, full:full + P], shared[0:1, full:full + P])
                            dve.tensor_copy(outs[r][:, 0:full], shared[:, 0:full]).then_inc(shared_read, 1)
                        elif kind in ("mean", "norm", "split"):
                            prepare(kind, x, n + 1, (k + 1) % 2, use(n, (kind, x)) if kind == "mean" else None)
                        elif kind == "choose":
                            choose(n + 1, x, use(n, ("route", 0)))

        @block.tensor
        def _(pe):
            pe.wait_ge(cleared, START + 1)

            def step(kind, x, slot, at, pair):
                if kind == "mean":
                    pe.wait_ge(squared, START + pair + 1)
                    pe.wait_ge(shared_read, START + at - 1)
                    pe.matmul(shared[:, 0:THIRD], chip.const(C_MEAN), third(squares, x), start=True, stop=True)\
                      .then_inc(shared_ready, 1)
                elif kind == "route":
                    pe.wait_ge(flat_ready, START + pair * 3 + 1)
                    pe.wait_ge(shared_read, START + at - 1)
                    for t in range(9):
                        first = min(t * P, TP - P)
                        ins = pe.matmul(shared[:, t * 16:(t + 1) * 16], flat[:, first:first + P],
                                        chip.router[:, :], start=True, stop=True)
                    ins.then_inc(shared_ready, 1)
                elif kind == "turn_weights":
                    pe.wait_ge(chosen, START + (pair + 1) * CHOSEN)
                    pe.wait_ge(shared_read, START + at - 1)
                    for t in range(TILES) if x == 0 else (TILES,):
                        col = t % TILES * P
                        ins = pe.transpose(shared[:, :].bitcast(BF16)[0:96, col:col + P],
                                           wparts[:, t * 96:(t + 1) * 96], chip.ident16[:, :])
                    ins.then_inc(shared_ready, 1)

            def up(n, x, slot):
                c, b, p, m = unit(x % UNITS)
                n_rows = CHUNKS[m][1]
                w = (p * 3 + m) * P
                if x % UNITS == 0:
                    pe.wait_ge(moved, START + n * 64 + 64 * (1 + x // UNITS))
                for read, bk, weights, got in ((gates, A_BANKS, chip.w1, up_a), (hiddens, B_BANKS, chip.w3, up_b)):
                    if x >= 2:
                        pe.wait_ge(read, START + n * UNITS + (x - 1))
                    for part in range(2):
                        at = part * (PAIRS * 3 * P) + w
                        ins = pe.matmul(bank[bk[x % 2]][0:n_rows, 0:THIRD], weights[:, at:at + n_rows],
                                        third(halves[slot][b], c), start=part == 0, stop=part == 1)
                    ins.then_inc(got, 1)

            for kind, x in E_PROLOGUE:
                if kind in E_SHARED_KINDS:
                    step(kind, x, 0, use_first((kind, x)), 0)
            for x in range(LAG):
                up(0, x, 0)
            with pe.Fori(0, turns) as i:
                for k in range(2):
                    n = pe.snap(2 * i + k)
                    for kind, x in E_ORDER:
                        if kind == "up":
                            up(n, x, (k + x // UNITS) % 2)
                        elif kind == "down":
                            c, b, p, m = unit(x)
                            rows_ = CHUNKS[m][1]
                            g = x // 3
                            outputs = (slice(0, D), slice(D, P), slice(0, P))[m]
                            w = (p * 3 + m) * P
                            pe.wait_ge(hiddens, START + n * UNITS + (x + 1))
                            if m == 0:
                                pe.wait_ge(weighs, START + n * GROUPS + max(g - 1, 0))
                            pe.matmul(bank[OUT_BANKS[g % 2]][outputs, 0:THIRD],
                                      chip.w2[0:rows_, w + outputs.start:w + outputs.stop],
                                      hidden[x % HIDDEN_RING][0:rows_, :], start=m < 2, stop=m == 2)\
                              .then_inc(downs, 1)
                        elif kind == "spread":
                            c, b, p, _ = unit(3 * x)
                            at = use(n, (kind, x))
                            pe.wait_ge(shared_read, START + at - 1)
                            w = (b * PAIRS + p) * P
                            pe.matmul(shared[:, 0:THIRD], chip.spread16[0:96, w:w + P], third(turned[k], c)[0:96],
                                      start=True, stop=True).then_inc(shared_ready, 1)
                        elif kind == "fold":
                            c, b = divmod(x, 2)
                            pe.wait_ge(adds, START + n * (ADDS * FOLDS) + (x + 1) * ADDS)
                            if b == 0:
                                pe.wait_ge(closes, START + n * 3 + c)
                            pe.matmul(total[D * b:D * (b + 1), 0:THIRD], chip.const(C_FOLD, D), added[x % 2][:, :],
                                      start=True, stop=True).then_inc(folds, 1)
                        elif kind == "emit":
                            at = use(n, (kind, x))
                            pe.wait_ge(closes, START + n * 3 + (x + 1))
                            pe.wait_ge(shared_read, START + at - 1)
                            for a, t in enumerate(EMIT_TILES[x]):
                                tokens = P if t < TILES else 2
                                ins = pe.transpose(shared[0:tokens, a * P:(a + 1) * P],
                                                   whole[:, t * P:t * P + tokens], chip.const(C_IDENT))
                            ins.then_inc(shared_ready, 1)
                        elif kind in E_SHARED_KINDS:
                            step(kind, x, (k + 1) % 2, use(n, (kind, x)), n + 1)


def build(nc, dram):
    images = dram["x"].shape[0]
    for name, n in (("h", 0), ("mixed", 0), ("h2", 2), ("z", 1), ("hn", AHEAD), ("x2", 2)):
        dram[name] = nc.dram_tensor("scratch_" + name, [images + n, D, TP], F32, kind="Internal").ap()
    with ExitStack() as ctx:
        chip = Chip(nc, ctx, images)
        load_weights(nc, chip, dram)
        mix(nc, chip, dram, images)
        normalize(nc, chip, dram, images)
        attend(nc, chip, dram, images)
        route_and_mix_experts(nc, chip, dram, images)


def kernel(**inputs):
    import numpy as np
    import concourse.bacc as bacc
    from concourse.bass_utils import run_bass_kernel_spmd

    nc = bacc.Bacc("TRN2", target_bir_lowering=False, num_devices=1)
    arrays = {name: np.ascontiguousarray(a) for name, a in inputs.items()}
    arrays["shape_consts"] = shape_constants()
    dram = {name: nc.dram_tensor(name, a.shape, mybir.dt.from_np(a.dtype), kind="ExternalInput").ap()
            for name, a in arrays.items()}
    images = arrays["x"].shape[0]
    dram["out"] = nc.dram_tensor("out", (images, T, D), F32, kind="ExternalOutput").ap()
    build(nc, dram)
    result = run_bass_kernel_spmd(nc, [arrays], core_ids=[0])
    return result.results[0]["out"]
```
